# Optimizing a Trainium2 kernel written in Bass

```python
import numpy as np
import jax
import jax.numpy as jnp

def _softmax(x, axis=-1):
    return jax.nn.softmax(x, axis=axis)

def _gelu(x):
    return jax.nn.gelu(x, approximate=True)

def _silu(x):
    return jax.nn.silu(x)

def _sigmoid(x):
    return jax.nn.sigmoid(x)

def _layernorm(x, axis=-1, eps=1e-05):
    m = jnp.mean(x, axis=axis, keepdims=True)
    v = jnp.var(x, axis=axis, keepdims=True)
    return (x - m) / jnp.sqrt(v + eps)

def _scatter_add(tgt, idx, src, axis=0):
    return tgt.at[idx].add(src)

def _segment_sum(src, seg, n):
    return jax.ops.segment_sum(src, seg, n)
kernel_name = 'mk_gnn_resnorm_d1_gnn_r8_8547be'

def setup_inputs(seed: int=0):
    np.random.seed(seed)
    _w = jnp.asarray

    def _rec_inputs():
        import jax
        import jax.numpy as jnp
        _gk = jax.random.key(seed)
        x = -0.0001006 + 1 * jax.random.normal(jax.random.fold_in(_gk, 1), (12500, 96), jnp.float32)
        _s = jax.random.randint(jax.random.fold_in(_gk, 2), (200000,), 0, 12500, jnp.int32)
        _d = jax.random.randint(jax.random.fold_in(_gk, 3), (200000,), 0, 12500, jnp.int32)
        _loop = jnp.arange(12500, dtype=jnp.int32)
        src = jnp.concatenate([_s, _d, _loop])
        dst = jnp.concatenate([_d, _s, _loop])
        _o = jnp.argsort(dst, stable=True)
        src = src[_o]
        dst = dst[_o]
        edge_attr_96 = 5.93493e-05 + 1.00006 * jax.random.normal(jax.random.fold_in(_gk, 11), (412500, 96), jnp.float32)
        return (x, src, dst, edge_attr_96)
    x, src, dst, edge_attr_96 = _rec_inputs()

    def _L0_gnn_setup():
        import jax, jax.numpy as jnp
        import numpy as np
        N_NODES = 6250
        N_EDGES = 100000
        IN_DIM = 96
        NUM_HEADS = 8
        HEAD_DIM = IN_DIM // NUM_HEADS
        key = jax.random.key(seed)
        ks = jax.random.split(key, 11)
        s = 1.0 / np.sqrt(IN_DIM)
        return {'x': jax.random.normal(ks[0], (N_NODES, IN_DIM), dtype=jnp.float32), 'edge_index': jax.random.randint(ks[1], (2, N_EDGES), 0, N_NODES, dtype=jnp.int64), 'edge_attr': jax.random.normal(ks[2], (N_EDGES, IN_DIM), dtype=jnp.float32), 'Wq': jax.random.normal(ks[3], (IN_DIM, IN_DIM), dtype=jnp.float32) * s, 'bq': jax.random.normal(ks[4], (IN_DIM,), dtype=jnp.float32) * s, 'Wk': jax.random.normal(ks[5], (IN_DIM, IN_DIM), dtype=jnp.float32) * s, 'bk': jax.random.normal(ks[6], (IN_DIM,), dtype=jnp.float32) * s, 'We': jax.random.normal(ks[7], (IN_DIM, IN_DIM), dtype=jnp.float32) * s, 'be': jax.random.normal(ks[8], (IN_DIM,), dtype=jnp.float32) * s, 'Wv': jax.random.normal(ks[9], (IN_DIM, IN_DIM), dtype=jnp.float32) * s, 'bv': jax.random.normal(ks[10], (IN_DIM,), dtype=jnp.float32) * s}
    _L0_gnn_all = _L0_gnn_setup()
    _L0_gnn_in = {k: v for k, v in _L0_gnn_all.items() if k in ('Wq', 'bq', 'Wk', 'bk', 'We', 'be', 'Wv', 'bv')}
    del _L0_gnn_all
    return {'x': x, 'src': src, 'dst': dst, 'edge_attr_96': edge_attr_96, 'L0_gnn_Wq': _L0_gnn_in['Wq'], 'L0_gnn_bq': _L0_gnn_in['bq'], 'L0_gnn_Wk': _L0_gnn_in['Wk'], 'L0_gnn_bk': _L0_gnn_in['bk'], 'L0_gnn_We': _L0_gnn_in['We'], 'L0_gnn_be': _L0_gnn_in['be'], 'L0_gnn_Wv': _L0_gnn_in['Wv'], 'L0_gnn_bv': _L0_gnn_in['bv']}

def reference(x, src, dst, edge_attr_96, L0_gnn_Wq, L0_gnn_bq, L0_gnn_Wk, L0_gnn_bk, L0_gnn_We, L0_gnn_be, L0_gnn_Wv, L0_gnn_bv):
    import jax
    import jax.numpy as jnp

    def _L0_gnn_ref(x, edge_index, edge_attr, Wq, bq, Wk, bk, We, be, Wv, bv):
        import jax, jax.numpy as jnp
        import numpy as np
        N_NODES = 6250
        N_EDGES = 100000
        IN_DIM = 96
        NUM_HEADS = 8
        HEAD_DIM = IN_DIM // NUM_HEADS
        N = x.shape[0]
        H, D = (NUM_HEADS, HEAD_DIM)
        Q_h = (x @ Wq + bq).reshape(N, H, D)
        K_h = (x @ Wk + bk).reshape(N, H, D)
        V_h = (x @ Wv + bv).reshape(N, H, D)
        E = (edge_attr @ We + be).reshape(-1, H, D)
        src_idx = edge_index[0]
        dst_idx = edge_index[1]
        src = K_h[src_idx]
        dest = Q_h[dst_idx]
        score = src * dest / jnp.sqrt(jnp.asarray(D, x.dtype))
        score = score * E
        score = jnp.exp(jnp.clip(score.sum(-1, keepdims=True), -5.0, 5.0))
        msg = V_h[src_idx] * score
        wV = jax.ops.segment_sum(msg, dst_idx, num_segments=N)
        Z = jax.ops.segment_sum(score, dst_idx, num_segments=N)
        h_out = wV / (Z + 1e-06)
        return h_out.reshape(N, H * D)
    edge_index = jnp.stack([src, dst])
    x = _layernorm(x + _L0_gnn_ref(x, edge_index, edge_attr_96, L0_gnn_Wq, L0_gnn_bq, L0_gnn_Wk, L0_gnn_bk, L0_gnn_We, L0_gnn_be, L0_gnn_Wv, L0_gnn_bv), axis=-1)
    return x

_drawn_inputs = setup_inputs


def setup_inputs(seed=0):
    import zlib

    import numpy as np

    out = dict(_drawn_inputs(seed))
    spreads = {}
    factors = {}
    for name, (base, spread) in spreads.items():
        noise = np.random.default_rng([zlib.crc32(name.encode()), seed]).standard_normal(out[name].shape)
        drawn = base * np.exp(spread * noise) if base else spread * noise
        out[name] = jnp.asarray(drawn.astype(out[name].dtype))
    for name, factor in factors.items():
        out[name] = (out[name] * factor).astype(out[name].dtype)
    return out
```

```python
from contextlib import ExitStack

import concourse.bass as bass
from concourse import mybir

ALU = mybir.AluOpType
ACT = mybir.ActivationFunctionType
AX_X = mybir.AxisListType.X
F32 = mybir.dt.float32
I32 = mybir.dt.int32

P = 128
HEADS = 8
G = 4
CHUNK = P * G
WIN = 32
WIN_SHIFT = 5
RING = 4
NP = 125
NP16 = 112
BATCH = 5
OUT_TILES = 4
NOWHERE = -1.0e6


def at_least(engine, sem, value):
    if not (isinstance(value, int) and value <= 0):
        engine.wait_ge(sem, value)


def run_steps(engine, step, chunks, lag):
    rounds = (chunks - 1) // RING
    for s in range(RING):
        step(s, s)
    with engine.Fori(1, rounds) as i:
        for u in range(RING):
            step(i * RING + u, u)
    for s in range(rounds * RING, chunks + lag):
        step(s, s % RING)


def gnn_kernel(nc, x, src, dst, edge_attr, Wq, bq, Wk, bk, We, be, Wv, bv, out):
    N, D = x.shape
    E = src.shape[0]
    HD = D // HEADS
    DA = D + 1
    DZ = D + HEADS
    C = (E + CHUNK - 1) // CHUNK
    FULL = E // CHUNK
    DUP = C * CHUNK - E
    NQ = 115
    NJ = FULL // NQ
    TILES = N // NP
    N_PAD = (N + WIN + P - 1) // P * P
    QSCALE = float(HD) ** -0.5
    EPS_LN = 1e-5
    assert NQ * NJ == FULL and FULL == C - 1 and NP * TILES == N and DUP % G == 0
    assert TILES % (4 * BATCH) == 0 and TILES % OUT_TILES == 0 and 1 << WIN_SHIFT == WIN
    assert CHUNK <= 512 and OUT_TILES * DZ <= 512 and NQ * G <= 512

    kv_dram = nc.dram_tensor("kv_table", (N, 2 * D), F32)
    q_dram = nc.dram_tensor("q_table", (N_PAD, D), F32)
    base_dram = nc.dram_tensor("chunk_base", (C,), I32)
    extra_dram = nc.dram_tensor("chunk_extra_windows", (C,), I32)

    with ExitStack() as ctx:
        def sb(name, shape, dt=F32):
            return ctx.enter_context(nc.sbuf_tensor(name, shape, dt))

        def sem(name):
            return ctx.enter_context(nc.semaphore(name))

        iota_i = sb("iota_i", [P, P], I32)
        part_i = sb("part_i", [P, 1], I32)
        iota = sb("iota", [P, P])
        part = sb("part", [P, 1])
        ident = sb("ident", [P, P])
        w_kvq = sb("w_kvq", [DA, 3 * D])
        w_e = sb("w_e", [DA, D])
        x_in = sb("x_in", [P, 2, BATCH, D])
        xT = sb("xT", [DA, 2, P])
        kv_out = sb("kv_out", [P, 2, BATCH, 2 * D])
        q_out = sb("q_out", [P, 2, BATCH, D])
        pad_rows = sb("pad_rows", [N_PAD - N, D])
        accT = sb("accT", [P, N_PAD])
        dst_nat = accT[0:NQ, 0:NJ * CHUNK]
        dst_end_row = sb("dst_end_row", [1, CHUNK], I32)
        dst_end = sb("dst_end", [P, G], I32)
        lohi = sb("lohi", [P, 4, NJ])
        lohi_i = sb("lohi_i", [P, 4, NJ], I32)
        lohi_end = sb("lohi_end", [1, 4])
        lohi_end_i = sb("lohi_end_i", [1, 4], I32)
        base_tab = sb("base_tab", [1, C], I32)
        extra_tab = sb("extra_tab", [1, C], I32)
        base_all = sb("base_all", [P, C], I32)
        node_id = sb("node_id", [WIN, C])
        rel = sb("rel", [P, C * G])
        ea = sb("ea", [P, RING, G, D])
        dst_b = sb("dst_b", [WIN, RING, CHUNK], I32)
        q_win = sb("q_win", [WIN, RING, D])
        src_idx = sb("src_idx", [P, RING, G], I32)
        kv = sb("kv", [P, RING, G, 2 * D])
        eaT = sb("eaT", [DA, 2, CHUNK])
        ohT = sb("ohT", [WIN, 2, CHUNK])
        oh = sb("oh", [P, 2, G, WIN])
        kqe = sb("kqe", [P, G, D])
        raw_score = sb("raw_score", [P, G * HEADS])
        score = sb("score", [P, 2, G * HEADS])
        msg = sb("msg", [P, 2, G, DZ])
        x_q_win = sb("x_q_win", [WIN, D])
        x_node_id = sb("x_node_id", [WIN, 1])
        x_ohT = sb("x_ohT", [WIN, CHUNK])
        x_rel = sb("x_rel", [P, G])
        x_oh = sb("x_oh", [P, G, WIN])
        accP = sb("accP", [DZ, 2, OUT_TILES, NP])
        x_res = sb("x_res", [P, 2, OUT_TILES, D])
        y = sb("y", [P, 2, OUT_TILES, D])
        ysq = sb("ysq", [P, 2, OUT_TILES, D])
        z_inv = sb("z_inv", [P, 2, OUT_TILES, HEADS])
        stat = sb("stat", [P, 2, 4, OUT_TILES])

        bank = [ctx.enter_context(nc.psum_tensor(f"bank{i}", [P, 512], F32)) for i in range(8)]
        eaT_ps, e_ps, q_ps, sum_ps = bank[0:2], bank[2:4], bank[4:6], bank[6:8]

        iota_made = sem("iota_made")
        ident_step = sem("ident_step")
        ident_ready = sem("ident_ready")
        ones_ready = sem("ones_ready")
        weights_in = sem("weights_in")
        dst_in = sem("dst_in")
        ends_in = sem("ends_in")
        pad_zeroed = sem("pad_zeroed")
        x_in_landed = [sem(f"x_in_landed{i}") for i in range(2)]
        x_turned = sem("x_turned")
        x_copied = sem("x_copied")
        kvq_done = sem("kvq_done")
        kv_evac = sem("kv_evac")
        q_evac = sem("q_evac")
        tables_stored = [sem(f"tables_stored{i}") for i in range(2)]
        range_step = sem("range_step")
        range_ready = sem("range_ready")
        range_stored = sem("range_stored")
        tabs_in = sem("tabs_in")
        node_id_ready = sem("node_id_ready")
        dst_turned = sem("dst_turned")
        rel_made = sem("rel_made")
        acc_zeroed = sem("acc_zeroed")
        ea_in = [sem(f"ea_in{i}") for i in range(RING)]
        dst_b_in = [sem(f"dst_b_in{i}") for i in range(RING)]
        q_win_in = [sem(f"q_win_in{i}") for i in range(RING)]
        src_idx_in = [sem(f"src_idx_in{i}") for i in range(RING)]
        slots_taken = sem("slots_taken")
        kv_in = [sem(f"kv_in{i}") for i in range(RING)]
        ea_turned = sem("ea_turned")
        eaT_copied = sem("eaT_copied")
        e_ready = sem("e_ready")
        ohT_built = sem("ohT_built")
        q_ready = sem("q_ready")
        kq_done = sem("kq_done")
        kqe_done = sem("kqe_done")
        heads_summed = sem("heads_summed")
        score_ready = sem("score_ready")
        exp_done = sem("exp_done")
        oh_built = sem("oh_built")
        msg_ready = sem("msg_ready")
        sums_ready = sem("sums_ready")
        acc_added = sem("acc_added")
        x_id_set = sem("x_id_set")
        x_load_go = sem("x_load_go")
        x_q_win_in = sem("x_q_win_in")
        x_ohT_built = sem("x_ohT_built")
        x_q_added = sem("x_q_added")
        x_rel_set = sem("x_rel_set")
        x_oh_built = sem("x_oh_built")
        x_sums_ready = sem("x_sums_ready")
        x_acc_added = sem("x_acc_added")
        accP_copied = sem("accP_copied")
        acc_turned = sem("acc_turned")
        x_res_in = [sem(f"x_res_in{i}") for i in range(2)]
        z_step = sem("z_step")
        y_step = sem("y_step")
        y_attended = sem("y_attended")
        y_centred = sem("y_centred")
        std_inverted = sem("std_inverted")
        squared = sem("squared")
        var_ready = sem("var_ready")
        rooted = sem("rooted")
        y_ready = sem("y_ready")
        y_stored = [sem(f"y_stored{i}") for i in range(2)]

        kv_t = kv_dram.rearrange("(p t) d -> p t d", t=TILES)
        q_t = q_dram[0:N, :].rearrange("(p t) d -> p t d", t=TILES)
        x_t = x.rearrange("(p t) d -> p t d", t=TILES)
        out_t = out.rearrange("(p t) d -> p t d", t=TILES)
        NODE_PARTS = [(0, NP16), (NP16, NP)]

        def landed(engine, sems, c, u, per_load):
            if isinstance(c, int):
                engine.wait_ge(sems[u], per_load * (c // RING + 1))
            else:
                engine.wait_ge(sems[u], (c - u) * (per_load // RING) + per_load)

        def within(node):
            return nc.s_assert_within(node, 0, N - 1, skip_runtime_bounds_check_because=
                                      "a chunk's windows end with the one that holds its greatest destination")

        block = ctx.enter_context(nc.Block())

        @block.sync
        def _(sp):
            sp.dma_start(dst_nat.bitcast(I32), dst[0:FULL * CHUNK].rearrange("(q r) -> q r", q=NQ)).then_inc(dst_in, 16)
            sp.dma_start(dst_end_row[:, :], dst[E - CHUNK:E].rearrange("(a r) -> a r", a=1)).then_inc(ends_in, 16)
            sp.dma_start(dst_end[:, :], dst[E - CHUNK:E].rearrange("(p g) -> p g", g=G)).then_inc(ends_in, 16)
            for k, (w, b) in enumerate(((Wk, bk), (Wv, bv), (Wq, bq))):
                sp.dma_start(w_kvq[0:D, k * D:(k + 1) * D], w[:, :]).then_inc(weights_in, 16)
                sp.dma_start(w_kvq[D:DA, k * D:(k + 1) * D],
                             b.rearrange("(a d) -> a d", a=1)).then_inc(weights_in, 16)
            sp.dma_start(w_e[0:D, :], We[:, :]).then_inc(weights_in, 16)
            sp.dma_start(w_e[D:DA, :], be.rearrange("(a d) -> a d", a=1)).then_inc(weights_in, 16)

            def load_x(b, h):
                for lo, hi in NODE_PARTS:
                    sp.dma_start(x_in[lo:hi, h, :, :], x_t[lo:hi, bass.ds(b * BATCH, BATCH), :]).then_inc(x_in_landed[h], 16)

            def store_tables(b, h):
                sp.wait_ge(kv_evac, (b + 1) * BATCH)
                sp.wait_ge(q_evac, (b + 1) * BATCH)
                for lo, hi in NODE_PARTS:
                    sp.dma_start(kv_t[lo:hi, bass.ds(b * BATCH, BATCH), :], kv_out[lo:hi, h, :, :]).then_inc(tables_stored[h], 16)
                    sp.dma_start(q_t[lo:hi, bass.ds(b * BATCH, BATCH), :], q_out[lo:hi, h, :, :]).then_inc(tables_stored[h], 16)

            load_x(0, 0)
            load_x(1, 1)
            batches = TILES // BATCH
            with sp.Fori(0, batches // 2 - 1) as i:
                for h in range(2):
                    b = i * 2 + h
                    sp.wait_ge(x_turned, (b + 1) * BATCH)
                    load_x(b + 2, h)
                    store_tables(b, h)
            for h in range(2):
                store_tables(batches - 2 + h, h)
            sp.wait_ge(pad_zeroed, 1)
            sp.dma_start(q_dram[N:N_PAD, :], pad_rows[:, :]).then_inc(tables_stored[0], 16)

            sp.wait_ge(range_ready, 1)
            sp.dma_start(base_dram[0:FULL].rearrange("(q j) -> q j", j=NJ), lohi_i[0:NQ, 0, :]).then_inc(range_stored, 16)
            sp.dma_start(extra_dram[0:FULL].rearrange("(q j) -> q j", j=NJ), lohi_i[0:NQ, 3, :]).then_inc(range_stored, 16)
            sp.dma_start(base_dram[FULL:C].rearrange("(a r) -> a r", a=1), lohi_end_i[:, 0:1]).then_inc(range_stored, 16)
            sp.dma_start(extra_dram[FULL:C].rearrange("(a r) -> a r", a=1), lohi_end_i[:, 3:4]).then_inc(range_stored, 16)
            sp.wait_ge(range_stored, 64)
            sp.dma_start(base_tab[:, :], base_dram.rearrange("(a c) -> a c", a=1)).then_inc(tabs_in, 16)
            sp.dma_start(extra_tab[:, :], extra_dram.rearrange("(a c) -> a c", a=1)).then_inc(tabs_in, 16)
            sp.dma_start(base_all[:, :], base_dram.rearrange("(a c) -> a c", a=1).to_broadcast((P, C))).then_inc(tabs_in, 16)
            sp.wait_ge(tabs_in, 48)
            sp.wait_ge(tables_stored[0], 16 * (4 * batches // 2 + 1))
            sp.wait_ge(tables_stored[1], 16 * (4 * batches // 2))

            def step(s, u):
                if not isinstance(s, int) or s < C:
                    first_edge = (E - CHUNK if s == C - 1 else s * CHUNK) if isinstance(s, int) else s * CHUNK
                    base = sp.value_load(base_tab[0:1, bass.ds(s, 1)], min_val=0, max_val=N - 1)
                    if not isinstance(s, int):
                        first_edge = sp.snap(first_edge)
                    at_least(sp, ea_turned, s - RING + 1)
                    at_least(sp, kq_done, s - RING + 1)
                    sp.dma_start(ea[:, u, :, :], edge_attr[bass.ds(first_edge, CHUNK), :].rearrange(
                        "(p g) d -> p g d", g=G)).then_inc(ea_in[u], 16)
                    sp.dma_start(dst_b[:, u, :], dst[bass.ds(first_edge, CHUNK)].rearrange(
                        "(a r) -> a r", a=1).to_broadcast((WIN, CHUNK))).then_inc(dst_b_in[u], 16)
                    at_least(sp, q_ready, s - RING + 1)
                    sp.dma_start(q_win[:, u, :], q_dram[bass.ds(base, WIN), :]).then_inc(q_win_in[u], 16)
                    if not isinstance(s, int) or s >= RING:
                        landed(sp, kv_in, s - RING, u, 16 * G)
                    sp.dma_start(src_idx[:, u, :], src[bass.ds(first_edge, CHUNK)].rearrange(
                        "(p g) -> p g", g=G)).then_inc(src_idx_in[u], 16)
                c = s - 3
                if isinstance(s, int) and not 0 <= c < C:
                    return
                extra = sp.value_load(extra_tab[0:1, bass.ds(c, 1)], min_val=0, max_val=N // WIN)
                with sp.If(extra > 0):
                    base = sp.value_load(base_tab[0:1, bass.ds(c, 1)], min_val=0, max_val=N - 1)
                    with sp.Fori(0, extra) as j:
                        sp.wait_ge(x_load_go, 1)
                        sp.sem_clear(x_load_go)
                        row = within(base + (j + 1) * WIN)
                        sp.dma_start(x_q_win[:, :], q_dram[bass.ds(row, WIN), :]).then_inc(x_q_win_in, 16)

            run_steps(sp, step, C, 3)

            out_batches = TILES // OUT_TILES

            def load_res(b, h):
                for lo, hi in NODE_PARTS:
                    sp.dma_start(x_res[lo:hi, h, :, :], x_t[lo:hi, bass.ds(b * OUT_TILES, OUT_TILES), :]).then_inc(x_res_in[h], 16)

            def store_y(b, h):
                sp.wait_ge(y_ready, b + 1)
                for lo, hi in NODE_PARTS:
                    sp.dma_start(out_t[lo:hi, bass.ds(b * OUT_TILES, OUT_TILES), :], ysq[lo:hi, h, :, :]).then_inc(y_stored[h], 16)

            load_res(0, 0)
            load_res(1, 1)
            with sp.Fori(0, (out_batches - 3) // 2) as i:
                for h in range(2):
                    store_y(i * 2 + h, h)
                    load_res(i * 2 + h + 2, h)
            store_y(out_batches - 3, 0)
            load_res(out_batches - 1, 0)
            store_y(out_batches - 2, 1)
            store_y(out_batches - 1, 0)
            sp.wait_ge(y_stored[0], 32 * ((out_batches + 1) // 2))
            sp.wait_ge(y_stored[1], 32 * (out_batches // 2))

        @block.gpsimd
        def _(pool):
            nc.gpsimd.iota(iota_i[:, :], pattern=[[1, P]], base=0, channel_multiplier=0).then_inc(iota_made, 1)
            nc.gpsimd.iota(part_i[:, :], pattern=[[0, 1]], base=0, channel_multiplier=1).then_inc(iota_made, 1)
            pool.wait_ge(iota_made, 2)
            nc.gpsimd.memset(xT[D:DA, :, :], 1.0).then_inc(ones_ready, 1)
            pool.wait_ge(ones_ready, 1)
            nc.gpsimd.memset(eaT[D:DA, :, :], 1.0).then_inc(ones_ready, 1)
            pool.wait_ge(ones_ready, 2)
            nc.gpsimd.memset(pad_rows[:, :], 0.0).then_inc(pad_zeroed, 1)
            pool.wait_ge(pad_zeroed, 1)
            pool.wait_ge(dst_turned, NJ)
            nc.gpsimd.memset(accT[:, :], 0.0).then_inc(acc_zeroed, 1)

            batches = TILES // BATCH
            pool.wait_ge(tables_stored[0], 16 * (4 * batches // 2 + 1))
            pool.wait_ge(tables_stored[1], 16 * (4 * batches // 2))

            def step(s, u):
                at_least(pool, msg_ready, s - RING + 1)
                pool.sem_inc(slots_taken, 1)
                pool.wait_ge(src_idx_in[u], 16)
                pool.sem_clear(src_idx_in[u])
                for g in range(G):
                    pool.indirect_dma_start(kv[:, u, g, :], None, kv_dram[:, :],
                                            bass.IndirectOffsetOnAxis(ap=src_idx[:, u, g:g + 1], axis=0)
                                            ).then_inc(kv_in[u], 16)

            run_steps(pool, step, C, 0)

        @block.tensor
        def _(pe):
            pe.wait_ge(ident_ready, 1)

            pe.wait_ge(range_step, 1)
            for j in range(NJ):
                at_least(pe, rel_made, j - 1)
                rows = dst_nat[:, j * CHUNK:(j + 1) * CHUNK].rearrange("q (p g) -> q g p", g=G)
                for g in range(G):
                    last = nc.tensor.transpose(bank[6 + j % 2][:, g * NQ:(g + 1) * NQ], rows[:, g, :], ident[0:NQ, 0:NQ])
                last.then_inc(dst_turned, 1)

            pe.wait_ge(ones_ready, 2)
            pe.wait_ge(weights_in, 16 * 8)

            def product(t, k):
                pe.wait_ge(x_copied, t + 1)
                at_least(pe, kv_evac, t - 1)
                at_least(pe, q_evac, t - 1)
                nc.tensor.matmul(bank[2 + k % 2][0:NP, 0:3 * D], xT[:, k % 2, 0:NP], w_kvq[:, :],
                                 start=True, stop=True).then_inc(kvq_done, 1)

            pair = 2 * BATCH

            def node_pair(i):
                for k in range(pair):
                    t = i * pair + k
                    h, j = k // BATCH, k % BATCH
                    if j == 0:
                        pe.wait_ge(x_in_landed[h], i * 32 + 32)
                    at_least(pe, x_copied, t - 1)
                    nc.tensor.transpose(bank[k % 2][0:D, 0:NP], x_in[0:NP, h, j, :],
                                        ident[0:NP, 0:NP]).then_inc(x_turned, 1)
                    if not (isinstance(t, int) and t == 0):
                        product(t - 1, k - 1 + pair)

            node_pair(0)
            with pe.Fori(1, TILES // pair) as i:
                node_pair(i)
            product(TILES - 1, TILES - 1)

            pe.wait_ge(kv_evac, TILES)
            pe.wait_ge(q_evac, TILES)
            pe.wait_ge(tabs_in, 48)

            def step(s, u):
                if not isinstance(s, int) or s < C:
                    landed(pe, ea_in, s, u, 16)
                    at_least(pe, eaT_copied, s - 1)
                    for g in range(G):
                        last = nc.tensor.transpose(eaT_ps[u % 2][0:D, g * P:(g + 1) * P], ea[:, u, g, :], ident[:, :])
                    last.then_inc(ea_turned, 1)
                c, v = s - 1, (u - 1) % RING
                if not isinstance(s, int) or 0 <= c < C:
                    pe.wait_ge(eaT_copied, c + 1)
                    at_least(pe, kqe_done, c - 1)
                    for g in range(G):
                        last = nc.tensor.matmul(e_ps[v % 2][:, g * D:(g + 1) * D], eaT[:, v % 2, g * P:(g + 1) * P],
                                                w_e[:, :], start=True, stop=True)
                    last.then_inc(e_ready, 1)
                    pe.wait_ge(ohT_built, c + 1)
                    landed(pe, q_win_in, c, v, 16)
                    sel = ohT[:, v % 2, :].rearrange("n (p g) -> n g p", g=G)
                    for g in range(G):
                        last = nc.tensor.matmul(q_ps[v % 2][:, g * D:(g + 1) * D], sel[:, g, :], q_win[:, v, :],
                                                start=(g == 0), stop=(g == G - 1), skip_group_check=True)
                    last.then_inc(q_ready, 1)
                    extra = pe.value_load(extra_tab[0:1, bass.ds(c, 1)], min_val=0, max_val=N // WIN)
                    with pe.If(extra > 0):
                        x_sel = x_ohT[:, :].rearrange("n (p g) -> n g p", g=G)
                        with pe.Fori(0, extra) as j:
                            pe.wait_ge(x_ohT_built, 1)
                            pe.sem_clear(x_ohT_built)
                            pe.wait_ge(x_q_win_in, 16)
                            pe.sem_clear(x_q_win_in)
                            for g in range(G):
                                last = nc.tensor.matmul(q_ps[v % 2][:, g * D:(g + 1) * D], x_sel[:, g, :], x_q_win[:, :],
                                                        start=False, stop=(g == G - 1), skip_group_check=True)
                            last.then_inc(x_q_added, 1)
                c, v = s - 3, (u - 3) % RING
                if not isinstance(s, int) or 0 <= c < C:
                    extra = pe.value_load(extra_tab[0:1, bass.ds(c, 1)], min_val=0, max_val=N // WIN)
                    with pe.If(extra > 0):
                        with pe.Fori(0, extra) as j:
                            pe.wait_ge(x_oh_built, 1)
                            pe.sem_clear(x_oh_built)
                            pe.wait_ge(msg_ready, c + 1)
                            at_least(pe, acc_added, c - 1)
                            for g in range(G):
                                last = nc.tensor.matmul(sum_ps[v % 2][0:DZ, 0:WIN], msg[:, v % 2, g, :], x_oh[:, g, :],
                                                        start=(g == 0), stop=(g == G - 1))
                            last.then_inc(x_sums_ready, 1)
                            pe.wait_ge(x_acc_added, 1)
                            pe.sem_clear(x_acc_added)
                    pe.wait_ge(msg_ready, c + 1)
                    pe.wait_ge(oh_built, c + 1)
                    at_least(pe, acc_added, c - 1)
                    for g in range(G):
                        last = nc.tensor.matmul(sum_ps[v % 2][0:DZ, 0:WIN], msg[:, v % 2, g, :], oh[:, v % 2, g, :],
                                                start=(g == 0), stop=(g == G - 1))
                    last.then_inc(sums_ready, 1)

            run_steps(pe, step, C, 3)

            out_batches = TILES // OUT_TILES

            def turn_back(b, h):
                pe.wait_ge(accP_copied, b + 1)
                at_least(pe, y_attended, b - 1)
                for j in range(OUT_TILES):
                    last = nc.tensor.transpose(bank[h][0:NP, j * DZ:(j + 1) * DZ], accP[:, h, j, :], ident[0:DZ, 0:DZ])
                last.then_inc(acc_turned, 1)

            turn_back(0, 0)
            turn_back(1, 1)
            with pe.Fori(1, out_batches // 2) as i:
                for h in range(2):
                    turn_back(i * 2 + h, h)
            turn_back(out_batches - 1, 0)

        @block.scalar
        def _(act):
            def node_tile(t, k):
                act.wait_ge(x_turned, t + 1)
                at_least(act, kvq_done, t - 1)
                nc.scalar.copy(xT[0:D, k % 2, 0:NP], bank[k % 2][0:D, 0:NP]).then_inc(x_copied, 1)

            def node_kv(t, k, stores):
                h, j = (k // BATCH) % 2, k % BATCH
                act.wait_ge(kvq_done, t + 1)
                if j == 0:
                    at_least(act, tables_stored[h], stores)
                nc.scalar.copy(kv_out[0:NP, h, j, :], bank[2 + k % 2][0:NP, 0:2 * D]).then_inc(kv_evac, 1)

            pair = 2 * BATCH
            for k in range(pair):
                node_tile(k, k)
                if k >= 1:
                    node_kv(k - 1, k - 1, 0)
            with act.Fori(1, TILES // pair) as i:
                for k in range(pair):
                    node_tile(i * pair + k, k)
                    if k == 0:
                        node_kv(i * pair - 1, pair - 1, 0)
                    else:
                        node_kv(i * pair + k - 1, k - 1, i * 64)
            node_kv(TILES - 1, pair - 1, 0)

            def step(s, u):
                if not isinstance(s, int) or s < C:
                    act.wait_ge(ea_turned, s + 1)
                    at_least(act, e_ready, s - 1)
                    nc.scalar.copy(eaT[0:D, u % 2, :], eaT_ps[u % 2][0:D, :]).then_inc(eaT_copied, 1)
                c, v = s - 2, (u - 2) % RING
                if not isinstance(s, int) or 0 <= c < C:
                    act.wait_ge(score_ready, c + 1)
                    at_least(act, acc_added, c - 1)
                    nc.scalar.activation(msg[:, v % 2, :, D:DZ],
                                         score[:, v % 2, :].rearrange("p (g h) -> p g h", g=G), ACT.Exp).then_inc(exp_done, 1)

            run_steps(act, step, C, 2)

            out_batches = TILES // OUT_TILES
            acc_cols = accT[0:DZ, 0:N].rearrange("f (p t) -> f t p", t=TILES)
            act.wait_ge(acc_added, C)

            def collect(b, h):
                at_least(act, acc_turned, b - 1)
                nc.scalar.copy(accP[:, h, :, :], acc_cols[:, bass.ds(b * OUT_TILES, OUT_TILES), :]).then_inc(accP_copied, 1)

            def norm(b, h):
                act.wait_ge(y_centred, b + 1)
                if isinstance(b, int) and b >= 2 or not isinstance(b, int):
                    act.wait_ge(y_stored[h], (b - h) * 16)
                nc.scalar.activation(ysq[0:NP, h, :, :], y[0:NP, h, :, :], ACT.Square).then_inc(squared, 1)
                act.wait_ge(var_ready, b + 1)
                nc.scalar.activation(stat[0:NP, h, 3, :], stat[0:NP, h, 2, :], ACT.Sqrt).then_inc(rooted, 1)

            collect(0, 0)
            for b in range(2):
                collect(b + 1, 1 - b)
                norm(b, b)
            with act.Fori(1, out_batches // 2) as i:
                for h in range(2):
                    collect(i * 2 + h + 1, 1 - h)
                    norm(i * 2 + h, h)
            norm(out_batches - 1, 0)

        @block.vector
        def _(dve):
            dve.wait_ge(iota_made, 2)
            nc.vector.tensor_copy(iota[:, :], iota_i[:, :]).then_inc(ident_step, 1)
            nc.vector.tensor_copy(part[:, :], part_i[:, :]).then_inc(ident_step, 1)
            dve.wait_ge(ident_step, 2)
            nc.vector.tensor_tensor(ident[:, :], iota[:, :], part[:, 0:1].to_broadcast((P, P)), ALU.is_equal).then_inc(ident_ready, 1)

            dve.wait_ge(dst_in, 16)
            nc.vector.tensor_copy(dst_nat, dst_nat.bitcast(I32)).then_inc(range_step, 1)
            dve.wait_ge(range_step, 1)
            rows = dst_nat.rearrange("q (j r) -> q j r", j=NJ)
            nc.vector.tensor_reduce(lohi[0:NQ, 0, :], rows, AX_X, ALU.min).then_inc(range_step, 1)
            nc.vector.tensor_reduce(lohi[0:NQ, 1, :], rows, AX_X, ALU.max).then_inc(range_step, 1)
            dve.wait_ge(ends_in, 32)
            nc.vector.tensor_reduce(lohi_end[:, 0:1], dst_end_row[:, :], AX_X, ALU.min).then_inc(range_step, 1)
            nc.vector.tensor_reduce(lohi_end[:, 1:2], dst_end_row[:, :], AX_X, ALU.max).then_inc(range_step, 1)
            dve.wait_ge(range_step, 5)
            nc.vector.tensor_copy(lohi_i[0:NQ, 0, :], lohi[0:NQ, 0, :]).then_inc(range_step, 1)
            nc.vector.tensor_tensor(lohi_i[0:NQ, 2, :], lohi[0:NQ, 1, :], lohi[0:NQ, 0, :], ALU.subtract).then_inc(range_step, 1)
            nc.vector.tensor_copy(lohi_end_i[:, 0:1], lohi_end[:, 0:1]).then_inc(range_step, 1)
            nc.vector.tensor_tensor(lohi_end_i[:, 2:3], lohi_end[:, 1:2], lohi_end[:, 0:1], ALU.subtract).then_inc(range_step, 1)
            dve.wait_ge(range_step, 9)
            nc.vector.tensor_scalar(lohi_i[0:NQ, 3, :], lohi_i[0:NQ, 2, :], WIN_SHIFT, None, ALU.logical_shift_right).then_inc(range_step, 1)
            dve.wait_ge(range_step, 10)
            nc.vector.tensor_scalar(lohi_end_i[:, 3:4], lohi_end_i[:, 2:3], WIN_SHIFT, None, ALU.logical_shift_right).then_inc(range_ready, 1)
            rel_v = rel[:, 0:FULL * G].rearrange("p (q j g) -> p q j g", j=NJ, g=G)
            for j in range(NJ):
                dve.wait_ge(dst_turned, j + 1)
                ps = bank[6 + j % 2][:, 0:G * NQ].rearrange("p (g q) -> p q g", g=G)
                nc.vector.tensor_copy(rel_v[:, :, j, :], ps).then_inc(rel_made, 1)
            nc.vector.tensor_copy(rel[:, FULL * G:C * G], dst_end[:, :]).then_inc(rel_made, 1)

            def node_q(t, k, stores):
                h, j = k // BATCH, k % BATCH
                dve.wait_ge(kvq_done, t + 1)
                dve.wait_ge(kv_evac, t + 1)
                if j == 0:
                    at_least(dve, tables_stored[h], stores)
                nc.vector.tensor_scalar(q_out[0:NP, h, j, :], bank[2 + k % 2][0:NP, 2 * D:3 * D], QSCALE, None,
                                        ALU.mult).then_inc(q_evac, 1)

            pair = 2 * BATCH
            for k in range(pair):
                node_q(k, k, 0)
            with dve.Fori(1, TILES // pair) as i:
                for k in range(pair):
                    node_q(i * pair + k, k, i * 64)

            dve.wait_ge(tabs_in, 48)
            dve.wait_ge(rel_made, NJ + 1)
            nc.vector.tensor_tensor(node_id[:, :], base_all[0:WIN, :], part[0:WIN, 0:1].to_broadcast((WIN, C)),
                                    ALU.add).then_inc(node_id_ready, 1)
            rel_cg = rel[:, :].rearrange("p (c g) -> p c g", g=G)
            nc.vector.tensor_tensor(rel_cg, rel_cg, base_all[:, :].unsqueeze(2).to_broadcast((P, C, G)),
                                    ALU.subtract).then_inc(node_id_ready, 1)
            dve.wait_ge(node_id_ready, 2)
            nc.vector.memset(rel[0:DUP // G, FULL * G:C * G], NOWHERE).then_inc(node_id_ready, 1)
            dve.wait_ge(node_id_ready, 3)
            dve.wait_ge(acc_zeroed, 1)

            def step(s, u):
                if not isinstance(s, int) or s < C:
                    landed(dve, dst_b_in, s, u, 16)
                    at_least(dve, q_ready, s - 1)
                    nc.vector.tensor_tensor(ohT[:, u % 2, :], dst_b[:, u, :], node_id[:, bass.ds(s, 1)].to_broadcast((WIN, CHUNK)),
                                            ALU.is_equal).then_inc(ohT_built, 1)
                c, v = s - 2, (u - 2) % RING
                if not isinstance(s, int) or 0 <= c < C:
                    dve.wait_ge(q_ready, c + 1)
                    extra = dve.value_load(extra_tab[0:1, bass.ds(c, 1)], min_val=0, max_val=N // WIN)
                    with dve.If(extra > 0):
                        nc.vector.tensor_copy(x_node_id[:, :], node_id[:, bass.ds(c, 1)]).then_inc(x_id_set, 1)
                        dve.wait_ge(x_id_set, 1)
                        dve.sem_clear(x_id_set)
                        with dve.Fori(0, extra) as j:
                            dve.sem_inc(x_load_go, 1)
                            nc.vector.tensor_scalar(x_node_id[:, :], x_node_id[:, :], float(WIN), None, ALU.add).then_inc(x_id_set, 1)
                            dve.wait_ge(x_id_set, 1)
                            dve.sem_clear(x_id_set)
                            nc.vector.tensor_tensor(x_ohT[:, :], dst_b[:, v, :], x_node_id[:, 0:1].to_broadcast((WIN, CHUNK)),
                                                    ALU.is_equal).then_inc(x_ohT_built, 1)
                            dve.wait_ge(x_q_added, 1)
                            dve.sem_clear(x_q_added)
                    landed(dve, kv_in, c, v, 16 * G)
                    at_least(dve, heads_summed, c)
                    nc.vector.tensor_tensor(kqe[:, :, :], kv[:, v, :, 0:D],
                                            q_ps[v % 2][:, 0:G * D].rearrange("p (g d) -> p g d", g=G), ALU.mult).then_inc(kq_done, 1)
                    dve.wait_ge(kq_done, c + 1)
                    dve.wait_ge(e_ready, c + 1)
                    nc.vector.tensor_tensor(kqe[:, :, :], kqe[:, :, :],
                                            e_ps[v % 2][:, 0:G * D].rearrange("p (g d) -> p g d", g=G), ALU.mult).then_inc(kqe_done, 1)
                    dve.wait_ge(kqe_done, c + 1)
                    at_least(dve, score_ready, c)
                    nc.vector.tensor_reduce(raw_score[:, :], kqe[:, :, :].rearrange("p g (h d) -> p (g h) d", d=HD),
                                            AX_X, ALU.add).then_inc(heads_summed, 1)
                    dve.wait_ge(heads_summed, c + 1)
                    at_least(dve, exp_done, c - 1)
                    nc.vector.tensor_scalar(score[:, v % 2, :], raw_score[:, :], -5.0, 5.0, ALU.max, ALU.min).then_inc(score_ready, 1)
                c, v = s - 3, (u - 3) % RING
                if not isinstance(s, int) or 0 <= c < C:
                    at_least(dve, sums_ready, c - 1)
                    nc.vector.tensor_tensor(oh[:, v % 2, :, :], iota[:, 0:WIN].unsqueeze(1).to_broadcast((P, G, WIN)),
                                            rel[:, bass.ds(c * G, G)].unsqueeze(2).to_broadcast((P, G, WIN)),
                                            ALU.is_equal).then_inc(oh_built, 1)
                    dve.wait_ge(exp_done, c + 1)
                    nc.vector.tensor_tensor(msg[:, v % 2, :, 0:D].rearrange("p g (h d) -> p g h d", d=HD),
                                            kv[:, v, :, D:2 * D].rearrange("p g (h d) -> p g h d", d=HD),
                                            msg[:, v % 2, :, D:DZ].unsqueeze(3).to_broadcast((P, G, HEADS, HD)),
                                            ALU.mult).then_inc(msg_ready, 1)
                c, v = s - 4, (u - 4) % RING
                if not isinstance(s, int) or 0 <= c < C:
                    base = dve.value_load(base_tab[0:1, bass.ds(c, 1)], min_val=0, max_val=N - 1)
                    extra = dve.value_load(extra_tab[0:1, bass.ds(c, 1)], min_val=0, max_val=N // WIN)
                    with dve.If(extra > 0):
                        nc.vector.tensor_copy(x_rel[:, :], rel[:, bass.ds(c * G, G)]).then_inc(x_rel_set, 1)
                        dve.wait_ge(x_rel_set, 1)
                        dve.sem_clear(x_rel_set)
                        with dve.Fori(0, extra) as j:
                            nc.vector.tensor_scalar(x_rel[:, :], x_rel[:, :], float(-WIN), None, ALU.add).then_inc(x_rel_set, 1)
                            dve.wait_ge(x_rel_set, 1)
                            dve.sem_clear(x_rel_set)
                            nc.vector.tensor_tensor(x_oh[:, :, :], iota[:, 0:WIN].unsqueeze(1).to_broadcast((P, G, WIN)),
                                                    x_rel[:, :].unsqueeze(2).to_broadcast((P, G, WIN)),
                                                    ALU.is_equal).then_inc(x_oh_built, 1)
                            dve.wait_ge(x_sums_ready, 1)
                            dve.sem_clear(x_sums_ready)
                            at_least(dve, acc_added, c)
                            col = within(base + (j + 1) * WIN)
                            acc = accT[0:DZ, bass.ds(col, WIN)]
                            nc.vector.tensor_tensor(acc, sum_ps[v % 2][0:DZ, 0:WIN], acc, ALU.add).then_inc(x_acc_added, 1)
                    dve.wait_ge(sums_ready, c + 1)
                    at_least(dve, acc_added, c)
                    acc = accT[0:DZ, bass.ds(base, WIN)]
                    nc.vector.tensor_tensor(acc, sum_ps[v % 2][0:DZ, 0:WIN], acc, ALU.add).then_inc(acc_added, 1)

            run_steps(dve, step, C, 4)

            out_batches = TILES // OUT_TILES

            def finish(b, h):
                dve.wait_ge(acc_turned, b + 1)
                sums = bank[h][0:NP, 0:OUT_TILES * DZ].rearrange("p (j f) -> p j f", f=DZ)
                zi, yb = z_inv[0:NP, h, :, :], y[0:NP, h, :, :]
                mean, var = stat[0:NP, h, 0, :], stat[0:NP, h, 1, :]
                nc.vector.tensor_scalar(zi, sums[:, :, D:DZ], 1e-6, None, ALU.add).then_inc(z_step, 1)
                dve.wait_ge(z_step, 2 * b + 1)
                nc.vector.reciprocal(zi, zi).then_inc(z_step, 1)
                dve.wait_ge(z_step, 2 * b + 2)
                nc.vector.tensor_tensor(yb.rearrange("p j (h d) -> p j h d", d=HD),
                                        sums[:, :, 0:D].rearrange("p j (h d) -> p j h d", d=HD),
                                        zi.unsqueeze(3).to_broadcast((NP, OUT_TILES, HEADS, HD)), ALU.mult).then_inc(y_attended, 1)
                dve.wait_ge(y_attended, b + 1)
                if isinstance(b, int):
                    dve.wait_ge(x_res_in[h], 32 * (b // 2 + 1))
                else:
                    dve.wait_ge(x_res_in[h], (b - h) * 16 + 32)
                nc.vector.tensor_tensor(yb, yb, x_res[0:NP, h, :, :], ALU.add).then_inc(y_step, 1)
                dve.wait_ge(y_step, 4 * b + 1)
                nc.vector.tensor_reduce(mean, yb, AX_X, ALU.add).then_inc(y_step, 1)
                dve.wait_ge(y_step, 4 * b + 2)
                nc.vector.tensor_scalar(mean, mean, 1.0 / D, None, ALU.mult).then_inc(y_step, 1)
                dve.wait_ge(y_step, 4 * b + 3)
                nc.vector.tensor_tensor(yb, yb, mean.unsqueeze(2).to_broadcast((NP, OUT_TILES, D)), ALU.subtract).then_inc(y_centred, 1)
                dve.wait_ge(squared, b + 1)
                nc.vector.tensor_reduce(var, ysq[0:NP, h, :, :], AX_X, ALU.add).then_inc(y_step, 1)
                dve.wait_ge(y_step, 4 * b + 4)
                nc.vector.tensor_scalar(stat[0:NP, h, 2, :], var, 1.0 / D, EPS_LN, ALU.mult, ALU.add).then_inc(var_ready, 1)
                dve.wait_ge(rooted, b + 1)
                nc.vector.reciprocal(stat[0:NP, h, 1, :], stat[0:NP, h, 3, :]).then_inc(std_inverted, 1)
                dve.wait_ge(std_inverted, b + 1)
                nc.vector.tensor_tensor(ysq[0:NP, h, :, :], yb,
                                        stat[0:NP, h, 1, :].unsqueeze(2).to_broadcast((NP, OUT_TILES, D)), ALU.mult).then_inc(y_ready, 1)

            with dve.Fori(0, out_batches // 2) as i:
                for h in range(2):
                    finish(i * 2 + h, h)
            finish(out_batches - 1, 0)


_INS = ['x', 'src', 'dst', 'edge_attr_96', 'L0_gnn_Wq', 'L0_gnn_bq', 'L0_gnn_Wk', 'L0_gnn_bk',
        'L0_gnn_We', 'L0_gnn_be', 'L0_gnn_Wv', 'L0_gnn_bv']


def kernel(**inputs):
    import numpy as _np
    import concourse.bacc as _bacc
    from concourse import mybir as _mybir
    from concourse.bass_utils import run_bass_kernel_spmd as _run

    nc = _bacc.Bacc("TRN2", target_bir_lowering=False, num_devices=1)
    arrays, args = {}, []
    for name in _INS:
        a = _np.ascontiguousarray(inputs[name])
        arrays[f"in_{name}_dram"] = a
        args.append(nc.dram_tensor(f"in_{name}_dram", a.shape, _mybir.dt.from_np(a.dtype), kind="ExternalInput").ap())
    args.append(nc.dram_tensor("out_0_dram", inputs["x"].shape, _mybir.dt.float32, kind="ExternalOutput").ap())
    gnn_kernel(nc, *args)
    r = _run(nc, [arrays], core_ids=[0])
    return r.results[0]["out_0_dram"]
```

```python
from contextlib import ExitStack

import concourse.bass as bass
from concourse import mybir

ALU = mybir.AluOpType
ACT = mybir.ActivationFunctionType
AX_X = mybir.AxisListType.X
F32 = mybir.dt.float32
BF16 = mybir.dt.bfloat16
I32 = mybir.dt.int32
I16 = mybir.dt.int16

P = 128
HEADS = 8
G = 4
CHUNK = P * G
WIN = 32
WIN_SHIFT = 5
PARTS = 3
SEL = WIN * PARTS
RING = 8
HALF = RING // 2
NP = 125
NP16 = 112
BATCH = 5
OUT_TILES = 4
NOWHERE = -1.0e6


def at_least(engine, sem, value):
    if not (isinstance(value, int) and value <= 0):
        engine.wait_ge(sem, value)


def run_steps(engine, step, chunks, lag, round_values=None):
    rounds = (chunks - 1) // RING
    extra_args = () if round_values is None else (None, True)
    for s in range(RING):
        step(s, s, *extra_args)
    with engine.Fori(1, rounds) as i:
        if round_values is None:
            for u in range(RING):
                step(i * RING + u, u)
        else:
            most, values = round_values(i)
            with engine.If(most > 0):
                for u in range(RING):
                    step(i * RING + u, u, values[u], True)
            with engine.Else():
                for u in range(RING):
                    step(i * RING + u, u, values[u], False)
    for s in range(rounds * RING, chunks + lag):
        step(s, s % RING, *extra_args)


def gnn_kernel(nc, x, src, dst, edge_attr, Wq, bq, Wk, bk, We, be, Wv, bv, out):
    N, D = x.shape
    E = src.shape[0]
    HD = D // HEADS
    DA = D + 1
    DZ = D + HEADS
    C = (E + CHUNK - 1) // CHUNK
    FULL = E // CHUNK
    DUP = C * CHUNK - E
    NQ = 115
    NJ = FULL // NQ
    ROUNDS = (C - 1) // RING
    TILES = N // NP
    N_PAD = (N + WIN + P - 1) // P * P
    QSCALE = float(HD) ** -0.5
    EPS_LN = 1e-5
    assert NQ * NJ == FULL and FULL == C - 1 and NP * TILES == N and DUP % G == 0
    assert TILES % (4 * BATCH) == 0 and TILES % OUT_TILES == 0 and 1 << WIN_SHIFT == WIN
    assert N_PAD < 1 << 15 and SEL <= P
    assert CHUNK <= 512 and OUT_TILES * DZ <= 512 and NQ * G <= 512

    kv_dram = nc.dram_tensor("kv_table", (N, 2 * D), F32)
    q_dram = nc.dram_tensor("q_table", (N_PAD * PARTS, D), BF16)
    dst16_dram = nc.dram_tensor("dst_by_chunk", (C * CHUNK,), I16)
    base_dram = nc.dram_tensor("chunk_base", (C,), I32)
    extra_dram = nc.dram_tensor("chunk_extra_windows", (C,), I32)

    with ExitStack() as ctx:
        def sb(name, shape, dt=F32):
            return ctx.enter_context(nc.sbuf_tensor(name, shape, dt))

        def sem(name):
            return ctx.enter_context(nc.semaphore(name))

        iota_i = sb("iota_i", [P, P], I32)
        part_i = sb("part_i", [P, 1], I32)
        iota = sb("iota", [P, P])
        part = sb("part", [P, 1])
        sel_row_i = sb("sel_row_i", [P, 1], I32)
        sel_row = sb("sel_row", [P, 1])
        ident = sb("ident", [P, P])
        w_kvq = sb("w_kvq", [DA, 3 * D])
        w_e = sb("w_e", [DA, D])
        x_in = sb("x_in", [P, 2, BATCH, D])
        xT = sb("xT", [DA, 2, P])
        kv_out = sb("kv_out", [P, 2, BATCH, 2 * D])
        q_f = sb("q_f", [P, 2, BATCH, D])
        q_rest = sb("q_rest", [P, BATCH, D])
        q_out = sb("q_out", [P, 2, BATCH, PARTS, D], BF16)
        pad_rows = sb("pad_rows", [N_PAD - N, PARTS * D], BF16)
        accT = sb("accT", [P, N_PAD])
        dst_nat = accT[0:NQ, 0:NJ * CHUNK]
        dst16 = sb("dst16", [NQ, NJ * CHUNK], I16)
        dst16_end = sb("dst16_end", [1, CHUNK], I16)
        dst_end_row = sb("dst_end_row", [1, CHUNK], I32)
        dst_end = sb("dst_end", [P, G], I32)
        lohi = sb("lohi", [P, 4, NJ])
        lohi_i = sb("lohi_i", [P, 4, NJ], I32)
        lohi_end = sb("lohi_end", [1, 4])
        lohi_end_i = sb("lohi_end_i", [1, 4], I32)
        base_tab = sb("base_tab", [1, C], I32)
        extra_tab = sb("extra_tab", [1, C], I32)
        round_most = sb("round_most", [1, ROUNDS], I32)
        rounds_most = sb("rounds_most", [1, ROUNDS], I32)
        base_all = sb("base_all", [P, C], I32)
        minus_id = sb("minus_id", [SEL, C])
        rel = sb("rel", [P, C * G])
        ea = sb("ea", [P, RING, G, D])
        dst_b = sb("dst_b", [SEL, RING, CHUNK], I16)
        q_win = sb("q_win", [SEL, RING, D], BF16)
        src_idx = sb("src_idx", [P, RING, G], I32)
        kv = sb("kv", [P, RING, G, 2 * D])
        eaT = sb("eaT", [DA, 2, CHUNK])
        away = sb("away", [SEL, CHUNK], BF16)
        ohT = sb("ohT", [SEL, 2, CHUNK], BF16)
        oh = sb("oh", [P, 2, G, WIN])
        kqe = sb("kqe", [P, G, D])
        raw_score = sb("raw_score", [P, G * HEADS])
        score = sb("score", [P, 2, G * HEADS])
        msg = sb("msg", [P, 2, G, DZ])
        x_q_win = sb("x_q_win", [SEL, D], BF16)
        x_node_id = sb("x_node_id", [SEL, 1])
        x_ohT = sb("x_ohT", [SEL, CHUNK], BF16)
        x_rel = sb("x_rel", [P, G])
        x_oh = sb("x_oh", [P, G, WIN])
        accP = sb("accP", [DZ, 2, OUT_TILES, NP])
        x_res = sb("x_res", [P, 2, OUT_TILES, D])
        y = sb("y", [P, 2, OUT_TILES, D])
        ysq = sb("ysq", [P, 2, OUT_TILES, D])
        z_inv = sb("z_inv", [P, 2, OUT_TILES, HEADS])
        stat = sb("stat", [P, 2, 4, OUT_TILES])

        bank = [ctx.enter_context(nc.psum_tensor(f"bank{i}", [P, 512], F32)) for i in range(8)]
        eaT_ps, e_ps, q_ps, sum_ps = bank[0:2], bank[2:4], bank[4:6], bank[6:8]

        iota_made = sem("iota_made")
        ident_step = sem("ident_step")
        ident_ready = sem("ident_ready")
        ones_ready = sem("ones_ready")
        weights_in = sem("weights_in")
        dst_in = sem("dst_in")
        ends_in = sem("ends_in")
        pad_zeroed = sem("pad_zeroed")
        x_in_landed = [sem(f"x_in_landed{i}") for i in range(2)]
        x_turned = sem("x_turned")
        x_copied = sem("x_copied")
        kvq_done = sem("kvq_done")
        kv_evac = sem("kv_evac")
        q_evac = sem("q_evac")
        q_split = sem("q_split")
        q_parts_ready = sem("q_parts_ready")
        tables_stored = [sem(f"tables_stored{i}") for i in range(2)]
        range_step = sem("range_step")
        range_ready = sem("range_ready")
        range_stored = sem("range_stored")
        dst16_made = sem("dst16_made")
        dst16_stored = sem("dst16_stored")
        tabs_in = sem("tabs_in")
        node_id_ready = sem("node_id_ready")
        dst_turned = sem("dst_turned")
        rel_made = sem("rel_made")
        most_step = sem("most_step")
        most_ready = sem("most_ready")
        acc_zeroed = sem("acc_zeroed")
        ea_in = [sem(f"ea_in{i}") for i in range(RING)]
        dst_b_in = [sem(f"dst_b_in{i}") for i in range(2)]
        q_win_in = [sem(f"q_win_in{i}") for i in range(RING)]
        src_idx_in = [sem(f"src_idx_in{i}") for i in range(2)]
        slots_taken = sem("slots_taken")
        kv_in = [sem(f"kv_in{i}") for i in range(RING)]
        ea_turned = sem("ea_turned")
        eaT_copied = sem("eaT_copied")
        e_ready = sem("e_ready")
        away_done = sem("away_done")
        ohT_built = sem("ohT_built")
        q_ready = sem("q_ready")
        kq_done = sem("kq_done")
        kqe_done = sem("kqe_done")
        heads_summed = sem("heads_summed")
        score_ready = sem("score_ready")
        exp_done = sem("exp_done")
        oh_built = sem("oh_built")
        msg_ready = sem("msg_ready")
        sums_ready = sem("sums_ready")
        acc_added = sem("acc_added")
        x_id_set = sem("x_id_set")
        x_load_go = sem("x_load_go")
        x_q_win_in = sem("x_q_win_in")
        x_ohT_built = sem("x_ohT_built")
        x_q_added = sem("x_q_added")
        x_rel_set = sem("x_rel_set")
        x_oh_built = sem("x_oh_built")
        x_sums_ready = sem("x_sums_ready")
        x_acc_added = sem("x_acc_added")
        accP_copied = sem("accP_copied")
        acc_turned = sem("acc_turned")
        x_res_in = [sem(f"x_res_in{i}") for i in range(2)]
        z_step = sem("z_step")
        y_step = sem("y_step")
        y_attended = sem("y_attended")
        y_centred = sem("y_centred")
        std_inverted = sem("std_inverted")
        squared = sem("squared")
        var_ready = sem("var_ready")
        rooted = sem("rooted")
        y_ready = sem("y_ready")
        y_stored = [sem(f"y_stored{i}") for i in range(2)]

        kv_t = kv_dram.rearrange("(p t) d -> p t d", t=TILES)
        q_t = q_dram[0:N * PARTS, :].rearrange("(p t k) d -> p t k d", t=TILES, k=PARTS)
        x_t = x.rearrange("(p t) d -> p t d", t=TILES)
        out_t = out.rearrange("(p t) d -> p t d", t=TILES)
        NODE_PARTS = [(0, NP16), (NP16, NP)]

        def landed_half(engine, c, u):
            if isinstance(c, int):
                engine.wait_ge(dst_b_in[u // HALF], 16 * (c // RING + 1))
            else:
                engine.wait_ge(dst_b_in[u // HALF], (c - u) * (16 // RING) + 16)

        def landed(engine, sems, c, u, per_load):
            if isinstance(c, int):
                engine.wait_ge(sems[u], per_load * (c // RING + 1))
            else:
                engine.wait_ge(sems[u], (c - u) * (per_load // RING) + per_load)

        IN_TAB = "these tables hold a chunk's least destination and how many further windows it has"

        def load_bases(engine, first):
            return nc.values_load_multi_w_load_instructions(
                base_tab[0:1, bass.ds(first, RING)], engines=(engine.engine,), min_val=0, max_val=N - 1,
                skip_runtime_bounds_check_because=IN_TAB)[1]

        def load_most(engine, i):
            return nc.values_load_multi_w_load_instructions(
                rounds_most[0:1, bass.ds(i, 1)], engines=(engine.engine,), min_val=0, max_val=N // WIN,
                skip_runtime_bounds_check_because=IN_TAB)[1][0]

        def within(node):
            return nc.s_assert_within(node, 0, N - 1, skip_runtime_bounds_check_because=
                                      "a chunk's windows end with the one that holds its greatest destination")

        block = ctx.enter_context(nc.Block())

        @block.sync
        def _(sp):
            sp.dma_start(dst_nat.bitcast(I32), dst[0:FULL * CHUNK].rearrange("(q r) -> q r", q=NQ)).then_inc(dst_in, 16)
            sp.dma_start(dst_end_row[:, :], dst[E - CHUNK:E].rearrange("(a r) -> a r", a=1)).then_inc(ends_in, 16)
            sp.dma_start(dst_end[:, :], dst[E - CHUNK:E].rearrange("(p g) -> p g", g=G)).then_inc(ends_in, 16)
            for k, (w, b) in enumerate(((Wk, bk), (Wv, bv), (Wq, bq))):
                sp.dma_start(w_kvq[0:D, k * D:(k + 1) * D], w[:, :]).then_inc(weights_in, 16)
                sp.dma_start(w_kvq[D:DA, k * D:(k + 1) * D],
                             b.rearrange("(a d) -> a d", a=1)).then_inc(weights_in, 16)
            sp.dma_start(w_e[0:D, :], We[:, :]).then_inc(weights_in, 16)
            sp.dma_start(w_e[D:DA, :], be.rearrange("(a d) -> a d", a=1)).then_inc(weights_in, 16)

            def load_x(b, h):
                for lo, hi in NODE_PARTS:
                    sp.dma_start(x_in[lo:hi, h, :, :], x_t[lo:hi, bass.ds(b * BATCH, BATCH), :]).then_inc(x_in_landed[h], 16)

            def store_tables(b, h):
                sp.wait_ge(kv_evac, (b + 1) * BATCH)
                sp.wait_ge(q_parts_ready, b + 1)
                for lo, hi in NODE_PARTS:
                    sp.dma_start(kv_t[lo:hi, bass.ds(b * BATCH, BATCH), :], kv_out[lo:hi, h, :, :]).then_inc(tables_stored[h], 16)
                    sp.dma_start(q_t[lo:hi, bass.ds(b * BATCH, BATCH), :, :], q_out[lo:hi, h, :, :, :]).then_inc(tables_stored[h], 16)

            load_x(0, 0)
            load_x(1, 1)
            batches = TILES // BATCH
            with sp.Fori(0, batches // 2 - 1) as i:
                for h in range(2):
                    b = i * 2 + h
                    sp.wait_ge(x_turned, (b + 1) * BATCH)
                    load_x(b + 2, h)
                    store_tables(b, h)
            for h in range(2):
                store_tables(batches - 2 + h, h)
            sp.wait_ge(pad_zeroed, 1)
            sp.dma_start(q_dram[N * PARTS:N_PAD * PARTS, :].rearrange("(n k) d -> n (k d)", k=PARTS), pad_rows[:, :]).then_inc(tables_stored[0], 16)

            sp.wait_ge(range_ready, 1)
            sp.dma_start(base_dram[0:FULL].rearrange("(q j) -> q j", j=NJ), lohi_i[0:NQ, 0, :]).then_inc(range_stored, 16)
            sp.dma_start(extra_dram[0:FULL].rearrange("(q j) -> q j", j=NJ), lohi_i[0:NQ, 3, :]).then_inc(range_stored, 16)
            sp.dma_start(base_dram[FULL:C].rearrange("(a r) -> a r", a=1), lohi_end_i[:, 0:1]).then_inc(range_stored, 16)
            sp.dma_start(extra_dram[FULL:C].rearrange("(a r) -> a r", a=1), lohi_end_i[:, 3:4]).then_inc(range_stored, 16)
            sp.wait_ge(range_stored, 64)
            sp.dma_start(base_tab[:, :], base_dram.rearrange("(a c) -> a c", a=1)).then_inc(tabs_in, 16)
            sp.dma_start(extra_tab[:, :], extra_dram.rearrange("(a c) -> a c", a=1)).then_inc(tabs_in, 16)
            sp.dma_start(base_all[:, :], base_dram.rearrange("(a c) -> a c", a=1).to_broadcast((P, C))).then_inc(tabs_in, 16)
            sp.wait_ge(dst16_made, 2)
            sp.dma_start(dst16_dram[0:FULL * CHUNK].rearrange("(q r) -> q r", q=NQ), dst16[:, :]).then_inc(dst16_stored, 16)
            sp.dma_start(dst16_dram[FULL * CHUNK:C * CHUNK].rearrange("(a r) -> a r", a=1), dst16_end[:, :]).then_inc(dst16_stored, 16)
            sp.wait_ge(dst16_stored, 32)
            sp.wait_ge(tabs_in, 48)
            sp.wait_ge(most_ready, 1)
            sp.wait_ge(tables_stored[0], 16 * (4 * batches // 2 + 1))
            sp.wait_ge(tables_stored[1], 16 * (4 * batches // 2))

            def load_indices(s, h):
                count = min(HALF, C - s) if isinstance(s, int) else HALF
                whole = count - 1 if isinstance(s, int) and s + count == C else count
                sp.dma_start(dst_b[:, h * HALF:h * HALF + count, :], dst16_dram[bass.ds(s * CHUNK, count * CHUNK)].rearrange(
                    "(a c r) -> a c r", a=1, c=count).to_broadcast((SEL, count, CHUNK))).then_inc(dst_b_in[h], 16)
                sp.dma_start(src_idx[:, h * HALF:h * HALF + whole, :], src[bass.ds(s * CHUNK, whole * CHUNK)].rearrange(
                    "(c p g) -> p c g", p=P, g=G)).then_inc(src_idx_in[h], 16)
                if whole < count:
                    sp.dma_start(src_idx[:, h * HALF + whole, :], src[E - CHUNK:E].rearrange(
                        "(p g) -> p g", g=G)).then_inc(src_idx_in[h], 16)

            def step(s, u, base, further):
                if not isinstance(s, int) or s < C:
                    first_edge = (E - CHUNK if s == C - 1 else s * CHUNK) if isinstance(s, int) else s * CHUNK
                    if base is None:
                        base = sp.value_load(base_tab[0:1, bass.ds(s, 1)], min_val=0, max_val=N - 1)
                    used = s - (HALF if u % HALF == 0 else RING - 1)
                    at_least(sp, ea_turned, used)
                    at_least(sp, kq_done, used)
                    sp.dma_start(ea[:, u, :, :], edge_attr[bass.ds(first_edge, CHUNK), :].rearrange(
                        "(p g) d -> p g d", g=G)).then_inc(ea_in[u], 16)
                    if u % HALF == 0:
                        load_indices(s, u // HALF)
                    sp.dma_start(q_win[:, u, :], q_dram[bass.ds(base * PARTS, SEL), :]).then_inc(q_win_in[u], 16)
                if not further:
                    return
                c = s - 3
                if isinstance(s, int) and not 0 <= c < C:
                    return
                extra = sp.value_load(extra_tab[0:1, bass.ds(c, 1)], min_val=0, max_val=N // WIN)
                with sp.If(extra > 0):
                    base = sp.value_load(base_tab[0:1, bass.ds(c, 1)], min_val=0, max_val=N - 1)
                    with sp.Fori(0, extra) as j:
                        sp.wait_ge(x_load_go, 1)
                        sp.sem_clear(x_load_go)
                        row = within(base + (j + 1) * WIN)
                        sp.dma_start(x_q_win[:, :], q_dram[bass.ds(row * PARTS, SEL), :]).then_inc(x_q_win_in, 16)

            run_steps(sp, step, C, 3, lambda i: (load_most(sp, i), load_bases(sp, i * RING)))

            out_batches = TILES // OUT_TILES

            def load_res(b, h):
                for lo, hi in NODE_PARTS:
                    sp.dma_start(x_res[lo:hi, h, :, :], x_t[lo:hi, bass.ds(b * OUT_TILES, OUT_TILES), :]).then_inc(x_res_in[h], 16)

            def store_y(b, h):
                sp.wait_ge(y_ready, b + 1)
                for lo, hi in NODE_PARTS:
                    sp.dma_start(out_t[lo:hi, bass.ds(b * OUT_TILES, OUT_TILES), :], ysq[lo:hi, h, :, :]).then_inc(y_stored[h], 16)

            load_res(0, 0)
            load_res(1, 1)
            with sp.Fori(0, (out_batches - 3) // 2) as i:
                for h in range(2):
                    store_y(i * 2 + h, h)
                    load_res(i * 2 + h + 2, h)
            store_y(out_batches - 3, 0)
            load_res(out_batches - 1, 0)
            store_y(out_batches - 2, 1)
            store_y(out_batches - 1, 0)
            sp.wait_ge(y_stored[0], 32 * ((out_batches + 1) // 2))
            sp.wait_ge(y_stored[1], 32 * (out_batches // 2))

        @block.gpsimd
        def _(pool):
            nc.gpsimd.iota(iota_i[:, :], pattern=[[1, P]], base=0, channel_multiplier=0).then_inc(iota_made, 1)
            nc.gpsimd.iota(part_i[:, :], pattern=[[0, 1]], base=0, channel_multiplier=1).then_inc(iota_made, 1)
            pool.wait_ge(iota_made, 2)
            nc.gpsimd.iota(sel_row_i[:, :], pattern=[[0, 1]], base=0,
                           channel_multiplier=(512 + PARTS - 1) // PARTS).then_inc(iota_made, 1)
            pool.wait_ge(iota_made, 3)
            nc.gpsimd.memset(xT[D:DA, :, :], 1.0).then_inc(ones_ready, 1)
            pool.wait_ge(ones_ready, 1)
            nc.gpsimd.memset(eaT[D:DA, :, :], 1.0).then_inc(ones_ready, 1)
            pool.wait_ge(ones_ready, 2)
            nc.gpsimd.memset(pad_rows[:, :], 0.0).then_inc(pad_zeroed, 1)
            pool.wait_ge(pad_zeroed, 1)
            pool.wait_ge(dst_turned, NJ)
            pool.wait_ge(dst16_made, 1)
            nc.gpsimd.memset(accT[:, :], 0.0).then_inc(acc_zeroed, 1)

            batches = TILES // BATCH
            pool.wait_ge(tables_stored[0], 16 * (4 * batches // 2 + 1))
            pool.wait_ge(tables_stored[1], 16 * (4 * batches // 2))

            def step(s, u):
                at_least(pool, msg_ready, s - RING + 1)
                pool.sem_inc(slots_taken, 1)
                if u % HALF == 0:
                    h = u // HALF
                    loads = 2 if isinstance(s, int) and s + HALF >= C else 1
                    pool.wait_ge(src_idx_in[h], 16 * loads)
                    pool.sem_clear(src_idx_in[h])
                for g in range(G):
                    pool.indirect_dma_start(kv[:, u, g, :], None, kv_dram[:, :],
                                            bass.IndirectOffsetOnAxis(ap=src_idx[:, u, g:g + 1], axis=0)
                                            ).then_inc(kv_in[u], 16)

            run_steps(pool, step, C, 0)

        @block.tensor
        def _(pe):
            pe.wait_ge(ident_ready, 1)

            pe.wait_ge(range_step, 1)
            for j in range(NJ):
                at_least(pe, rel_made, j - 1)
                rows = dst_nat[:, j * CHUNK:(j + 1) * CHUNK].rearrange("q (p g) -> q g p", g=G)
                for g in range(G):
                    last = nc.tensor.transpose(bank[6 + j % 2][:, g * NQ:(g + 1) * NQ], rows[:, g, :], ident[0:NQ, 0:NQ])
                last.then_inc(dst_turned, 1)

            pe.wait_ge(ones_ready, 2)
            pe.wait_ge(weights_in, 16 * 8)

            def product(t, k):
                pe.wait_ge(x_copied, t + 1)
                at_least(pe, kv_evac, t - 1)
                at_least(pe, q_evac, t - 1)
                nc.tensor.matmul(bank[2 + k % 2][0:NP, 0:3 * D], xT[:, k % 2, 0:NP], w_kvq[:, :],
                                 start=True, stop=True).then_inc(kvq_done, 1)

            pair = 2 * BATCH

            def node_pair(i):
                for k in range(pair):
                    t = i * pair + k
                    h, j = k // BATCH, k % BATCH
                    if j == 0:
                        pe.wait_ge(x_in_landed[h], i * 32 + 32)
                    at_least(pe, x_copied, t - 1)
                    nc.tensor.transpose(bank[k % 2][0:D, 0:NP], x_in[0:NP, h, j, :],
                                        ident[0:NP, 0:NP]).then_inc(x_turned, 1)
                    if not (isinstance(t, int) and t == 0):
                        product(t - 1, k - 1 + pair)

            node_pair(0)
            with pe.Fori(1, TILES // pair) as i:
                node_pair(i)
            product(TILES - 1, TILES - 1)

            pe.wait_ge(kv_evac, TILES)
            pe.wait_ge(q_evac, TILES)
            pe.wait_ge(most_ready, 1)

            def step(s, u, _, further):
                if not isinstance(s, int) or s < C:
                    landed(pe, ea_in, s, u, 16)
                    at_least(pe, eaT_copied, s - 1)
                    for g in range(G):
                        last = nc.tensor.transpose(eaT_ps[u % 2][0:D, g * P:(g + 1) * P], ea[:, u, g, :], ident[:, :])
                    last.then_inc(ea_turned, 1)
                c, v = s - 1, (u - 1) % RING
                if not isinstance(s, int) or 0 <= c < C:
                    pe.wait_ge(eaT_copied, c + 1)
                    at_least(pe, kqe_done, c - 1)
                    for g in range(G):
                        last = nc.tensor.matmul(e_ps[v % 2][:, g * D:(g + 1) * D], eaT[:, v % 2, g * P:(g + 1) * P],
                                                w_e[:, :], start=True, stop=True)
                    last.then_inc(e_ready, 1)
                    pe.wait_ge(ohT_built, c + 1)
                    landed(pe, q_win_in, c, v, 16)
                    sel = ohT[:, v % 2, :].rearrange("n (p g) -> n g p", g=G)
                    for g in range(G):
                        last = nc.tensor.matmul(q_ps[v % 2][:, g * D:(g + 1) * D], sel[:, g, :], q_win[:, v, :],
                                                start=(g == 0), stop=(g == G - 1), skip_group_check=True)
                    last.then_inc(q_ready, 1)
                    if further:
                        extra = pe.value_load(extra_tab[0:1, bass.ds(c, 1)], min_val=0, max_val=N // WIN)
                        with pe.If(extra > 0):
                            x_sel = x_ohT[:, :].rearrange("n (p g) -> n g p", g=G)
                            with pe.Fori(0, extra) as j:
                                pe.wait_ge(x_ohT_built, 1)
                                pe.sem_clear(x_ohT_built)
                                pe.wait_ge(x_q_win_in, 16)
                                pe.sem_clear(x_q_win_in)
                                for g in range(G):
                                    last = nc.tensor.matmul(q_ps[v % 2][:, g * D:(g + 1) * D], x_sel[:, g, :], x_q_win[:, :],
                                                            start=False, stop=(g == G - 1), skip_group_check=True)
                                last.then_inc(x_q_added, 1)
                c, v = s - 3, (u - 3) % RING
                if not isinstance(s, int) or 0 <= c < C:
                    if further:
                        extra = pe.value_load(extra_tab[0:1, bass.ds(c, 1)], min_val=0, max_val=N // WIN)
                        with pe.If(extra > 0):
                            with pe.Fori(0, extra) as j:
                                pe.wait_ge(x_oh_built, 1)
                                pe.sem_clear(x_oh_built)
                                pe.wait_ge(msg_ready, c + 1)
                                at_least(pe, acc_added, c - 1)
                                for g in range(G):
                                    last = nc.tensor.matmul(sum_ps[v % 2][0:DZ, 0:WIN], msg[:, v % 2, g, :], x_oh[:, g, :],
                                                            start=(g == 0), stop=(g == G - 1))
                                last.then_inc(x_sums_ready, 1)
                                pe.wait_ge(x_acc_added, 1)
                                pe.sem_clear(x_acc_added)
                    pe.wait_ge(msg_ready, c + 1)
                    pe.wait_ge(oh_built, c + 1)
                    at_least(pe, acc_added, c - 1)
                    for g in range(G):
                        last = nc.tensor.matmul(sum_ps[v % 2][0:DZ, 0:WIN], msg[:, v % 2, g, :], oh[:, v % 2, g, :],
                                                start=(g == 0), stop=(g == G - 1))
                    last.then_inc(sums_ready, 1)

            run_steps(pe, step, C, 3, lambda i: (load_most(pe, i), [None] * RING))

            out_batches = TILES // OUT_TILES

            def turn_back(b, h):
                pe.wait_ge(accP_copied, b + 1)
                at_least(pe, y_attended, b - 1)
                for j in range(OUT_TILES):
                    last = nc.tensor.transpose(bank[h][0:NP, j * DZ:(j + 1) * DZ], accP[:, h, j, :], ident[0:DZ, 0:DZ])
                last.then_inc(acc_turned, 1)

            turn_back(0, 0)
            turn_back(1, 1)
            with pe.Fori(1, out_batches // 2) as i:
                for h in range(2):
                    turn_back(i * 2 + h, h)
            turn_back(out_batches - 1, 0)

        @block.scalar
        def _(act):
            def node_tile(t, k):
                act.wait_ge(x_turned, t + 1)
                at_least(act, kvq_done, t - 1)
                nc.scalar.copy(xT[0:D, k % 2, 0:NP], bank[k % 2][0:D, 0:NP]).then_inc(x_copied, 1)

            def node_kv(t, k, stores):
                h, j = (k // BATCH) % 2, k % BATCH
                act.wait_ge(kvq_done, t + 1)
                if j == 0:
                    at_least(act, tables_stored[h], stores)
                nc.scalar.copy(kv_out[0:NP, h, j, :], bank[2 + k % 2][0:NP, 0:2 * D]).then_inc(kv_evac, 1)

            pair = 2 * BATCH
            for k in range(pair):
                node_tile(k, k)
                if k >= 1:
                    node_kv(k - 1, k - 1, 0)
            with act.Fori(1, TILES // pair) as i:
                for k in range(pair):
                    node_tile(i * pair + k, k)
                    if k == 0:
                        node_kv(i * pair - 1, pair - 1, 0)
                    else:
                        node_kv(i * pair + k - 1, k - 1, i * 64)
            node_kv(TILES - 1, pair - 1, 0)

            act.wait_ge(node_id_ready, 1)

            def step(s, u):
                if not isinstance(s, int) or s < C:
                    act.wait_ge(ea_turned, s + 1)
                    at_least(act, e_ready, s - 1)
                    nc.scalar.copy(eaT[0:D, u % 2, :], eaT_ps[u % 2][0:D, :]).then_inc(eaT_copied, 1)
                    if u % HALF == 0:
                        landed_half(act, s, u)
                    at_least(act, ohT_built, s)
                    nc.scalar.activation(away[:, :], dst_b[:, u, :], ACT.Abs,
                                         bias=minus_id[:, bass.ds(s, 1)]).then_inc(away_done, 1)
                    act.wait_ge(away_done, s + 1)
                    at_least(act, q_ready, s - 1)
                    nc.scalar.activation(ohT[:, u % 2, :], away[:, :], ACT.Relu, bias=1.0, scale=-1.0).then_inc(ohT_built, 1)
                c, v = s - 2, (u - 2) % RING
                if not isinstance(s, int) or 0 <= c < C:
                    act.wait_ge(score_ready, c + 1)
                    at_least(act, acc_added, c - 1)
                    nc.scalar.activation(msg[:, v % 2, :, D:DZ],
                                         score[:, v % 2, :].rearrange("p (g h) -> p g h", g=G), ACT.Exp).then_inc(exp_done, 1)

            run_steps(act, step, C, 2)

            out_batches = TILES // OUT_TILES
            acc_cols = accT[0:DZ, 0:N].rearrange("f (p t) -> f t p", t=TILES)
            act.wait_ge(acc_added, C)

            def collect(b, h):
                at_least(act, acc_turned, b - 1)
                nc.scalar.copy(accP[:, h, :, :], acc_cols[:, bass.ds(b * OUT_TILES, OUT_TILES), :]).then_inc(accP_copied, 1)

            def norm(b, h):
                act.wait_ge(y_centred, b + 1)
                if isinstance(b, int) and b >= 2 or not isinstance(b, int):
                    act.wait_ge(y_stored[h], (b - h) * 16)
                nc.scalar.activation(ysq[0:NP, h, :, :], y[0:NP, h, :, :], ACT.Square).then_inc(squared, 1)
                act.wait_ge(var_ready, b + 1)
                nc.scalar.activation(stat[0:NP, h, 3, :], stat[0:NP, h, 2, :], ACT.Sqrt).then_inc(rooted, 1)

            collect(0, 0)
            for b in range(2):
                collect(b + 1, 1 - b)
                norm(b, b)
            with act.Fori(1, out_batches // 2) as i:
                for h in range(2):
                    collect(i * 2 + h + 1, 1 - h)
                    norm(i * 2 + h, h)
            norm(out_batches - 1, 0)

        @block.vector
        def _(dve):
            dve.wait_ge(iota_made, 3)
            nc.vector.tensor_copy(iota[:, :], iota_i[:, :]).then_inc(ident_step, 1)
            nc.vector.tensor_copy(part[:, :], part_i[:, :]).then_inc(ident_step, 1)
            nc.vector.tensor_scalar(sel_row_i[:, :], sel_row_i[:, :], 9, None, ALU.logical_shift_right).then_inc(ident_step, 1)
            dve.wait_ge(ident_step, 3)
            nc.vector.tensor_copy(sel_row[:, :], sel_row_i[:, :]).then_inc(ident_step, 1)
            nc.vector.tensor_tensor(ident[:, :], iota[:, :], part[:, 0:1].to_broadcast((P, P)), ALU.is_equal).then_inc(ident_ready, 1)

            dve.wait_ge(dst_in, 16)
            nc.vector.tensor_copy(dst_nat, dst_nat.bitcast(I32)).then_inc(range_step, 1)
            dve.wait_ge(range_step, 1)
            rows = dst_nat.rearrange("q (j r) -> q j r", j=NJ)
            nc.vector.tensor_reduce(lohi[0:NQ, 0, :], rows, AX_X, ALU.min).then_inc(range_step, 1)
            nc.vector.tensor_reduce(lohi[0:NQ, 1, :], rows, AX_X, ALU.max).then_inc(range_step, 1)
            dve.wait_ge(ends_in, 32)
            nc.vector.tensor_reduce(lohi_end[:, 0:1], dst_end_row[:, :], AX_X, ALU.min).then_inc(range_step, 1)
            nc.vector.tensor_reduce(lohi_end[:, 1:2], dst_end_row[:, :], AX_X, ALU.max).then_inc(range_step, 1)
            dve.wait_ge(range_step, 5)
            nc.vector.tensor_copy(lohi_i[0:NQ, 0, :], lohi[0:NQ, 0, :]).then_inc(range_step, 1)
            nc.vector.tensor_tensor(lohi_i[0:NQ, 2, :], lohi[0:NQ, 1, :], lohi[0:NQ, 0, :], ALU.subtract).then_inc(range_step, 1)
            nc.vector.tensor_copy(lohi_end_i[:, 0:1], lohi_end[:, 0:1]).then_inc(range_step, 1)
            nc.vector.tensor_tensor(lohi_end_i[:, 2:3], lohi_end[:, 1:2], lohi_end[:, 0:1], ALU.subtract).then_inc(range_step, 1)
            dve.wait_ge(range_step, 9)
            nc.vector.tensor_scalar(lohi_i[0:NQ, 3, :], lohi_i[0:NQ, 2, :], WIN_SHIFT, None, ALU.logical_shift_right).then_inc(range_step, 1)
            dve.wait_ge(range_step, 10)
            nc.vector.tensor_scalar(lohi_end_i[:, 3:4], lohi_end_i[:, 2:3], WIN_SHIFT, None, ALU.logical_shift_right).then_inc(range_ready, 1)
            nc.vector.tensor_copy(dst16[:, :], dst_nat).then_inc(dst16_made, 1)
            nc.vector.tensor_copy(dst16_end[:, :], dst_end_row[:, :]).then_inc(dst16_made, 1)

            rel_v = rel[:, 0:FULL * G].rearrange("p (q j g) -> p q j g", j=NJ, g=G)
            for j in range(NJ):
                dve.wait_ge(dst_turned, j + 1)
                ps = bank[6 + j % 2][:, 0:G * NQ].rearrange("p (g q) -> p q g", g=G)
                nc.vector.tensor_copy(rel_v[:, :, j, :], ps).then_inc(rel_made, 1)
            nc.vector.tensor_copy(rel[:, FULL * G:C * G], dst_end[:, :]).then_inc(rel_made, 1)

            def node_q(t, k, stores, splits):
                h, j = k // BATCH, k % BATCH
                dve.wait_ge(kvq_done, t + 1)
                dve.wait_ge(kv_evac, t + 1)
                nc.vector.tensor_scalar(q_f[0:NP, h, j, :], bank[2 + k % 2][0:NP, 2 * D:3 * D], QSCALE, None,
                                        ALU.mult).then_inc(q_evac, 1)
                if j == BATCH - 1:
                    q, rest = q_f[0:NP, h, :, :], q_rest[0:NP, :, :]
                    parts = [q_out[0:NP, h, :, i, :] for i in range(PARTS)]
                    done = (t + 1 - BATCH) // BATCH * 3 if isinstance(t, int) else splits
                    dve.wait_ge(q_evac, t + 1)
                    at_least(dve, tables_stored[h], stores)
                    nc.vector.tensor_copy(parts[0], q).then_inc(q_split, 1)
                    dve.wait_ge(q_split, done + 1)
                    at_least(dve, q_parts_ready, done // 3)
                    nc.vector.tensor_tensor(rest, q, parts[0], ALU.subtract).then_inc(q_split, 1)
                    dve.wait_ge(q_split, done + 2)
                    nc.vector.tensor_copy(parts[1], rest).then_inc(q_split, 1)
                    dve.wait_ge(q_split, done + 3)
                    nc.vector.tensor_tensor(parts[2], rest, parts[1], ALU.subtract).then_inc(q_parts_ready, 1)

            pair = 2 * BATCH
            for k in range(pair):
                node_q(k, k, 0, 0)
            with dve.Fori(1, TILES // pair) as i:
                for k in range(pair):
                    node_q(i * pair + k, k, i * 64, i * 6 + k // BATCH * 3)

            dve.wait_ge(tabs_in, 48)
            nc.vector.tensor_reduce(round_most[:, :], extra_tab[:, 0:ROUNDS * RING].rearrange("a (i c) -> a i c", c=RING),
                                    AX_X, ALU.max).then_inc(most_step, 1)
            dve.wait_ge(most_step, 1)
            nc.vector.tensor_tensor(rounds_most[:, 1:ROUNDS], round_most[:, 0:ROUNDS - 1], round_most[:, 1:ROUNDS],
                                    ALU.max).then_inc(most_ready, 1)
            dve.wait_ge(most_ready, 1)
            dve.wait_ge(rel_made, NJ + 1)
            nc.vector.tensor_scalar(minus_id[:, :], base_all[0:SEL, :], sel_row[0:SEL, 0:1], -1.0,
                                    ALU.add, ALU.mult).then_inc(node_id_ready, 1)
            rel_cg = rel[:, :].rearrange("p (c g) -> p c g", g=G)
            nc.vector.tensor_tensor(rel_cg, rel_cg, base_all[:, :].unsqueeze(2).to_broadcast((P, C, G)),
                                    ALU.subtract).then_inc(node_id_ready, 1)
            dve.wait_ge(node_id_ready, 2)
            nc.vector.memset(rel[0:DUP // G, FULL * G:C * G], NOWHERE).then_inc(node_id_ready, 1)
            dve.wait_ge(node_id_ready, 3)
            dve.wait_ge(acc_zeroed, 1)

            def further_q(c, v):
                extra = dve.value_load(extra_tab[0:1, bass.ds(c, 1)], min_val=0, max_val=N // WIN)
                with dve.If(extra > 0):
                    nc.vector.tensor_scalar(x_node_id[:, :], minus_id[:, bass.ds(c, 1)], -1.0, None, ALU.mult).then_inc(x_id_set, 1)
                    dve.wait_ge(x_id_set, 1)
                    dve.sem_clear(x_id_set)
                    with dve.Fori(0, extra) as j:
                        dve.sem_inc(x_load_go, 1)
                        nc.vector.tensor_scalar(x_node_id[:, :], x_node_id[:, :], float(WIN), None, ALU.add).then_inc(x_id_set, 1)
                        dve.wait_ge(x_id_set, 1)
                        dve.sem_clear(x_id_set)
                        nc.vector.tensor_tensor(x_ohT[:, :], dst_b[:, v, :], x_node_id[:, 0:1].to_broadcast((SEL, CHUNK)),
                                                ALU.is_equal).then_inc(x_ohT_built, 1)
                        dve.wait_ge(x_q_added, 1)
                        dve.sem_clear(x_q_added)

            def further_sums(c, v, base):
                extra = dve.value_load(extra_tab[0:1, bass.ds(c, 1)], min_val=0, max_val=N // WIN)
                with dve.If(extra > 0):
                    nc.vector.tensor_copy(x_rel[:, :], rel[:, bass.ds(c * G, G)]).then_inc(x_rel_set, 1)
                    dve.wait_ge(x_rel_set, 1)
                    dve.sem_clear(x_rel_set)
                    with dve.Fori(0, extra) as j:
                        nc.vector.tensor_scalar(x_rel[:, :], x_rel[:, :], float(-WIN), None, ALU.add).then_inc(x_rel_set, 1)
                        dve.wait_ge(x_rel_set, 1)
                        dve.sem_clear(x_rel_set)
                        nc.vector.tensor_tensor(x_oh[:, :, :], iota[:, 0:WIN].unsqueeze(1).to_broadcast((P, G, WIN)),
                                                x_rel[:, :].unsqueeze(2).to_broadcast((P, G, WIN)),
                                                ALU.is_equal).then_inc(x_oh_built, 1)
                        dve.wait_ge(x_sums_ready, 1)
                        dve.sem_clear(x_sums_ready)
                        at_least(dve, acc_added, c)
                        col = within(base + (j + 1) * WIN)
                        acc = accT[0:DZ, bass.ds(col, WIN)]
                        nc.vector.tensor_tensor(acc, sum_ps[v % 2][0:DZ, 0:WIN], acc, ALU.add).then_inc(x_acc_added, 1)

            def step(s, u, base, further):
                a, m, n = s - 2, s - 3, s - 4
                ua, um, un = (u - 2) % RING, (u - 3) % RING, (u - 4) % RING
                scores = not isinstance(s, int) or 0 <= a < C
                messages = not isinstance(s, int) or 0 <= m < C
                sums = not isinstance(s, int) or 0 <= n < C
                if scores:
                    dve.wait_ge(q_ready, a + 1)
                    if further:
                        further_q(a, ua)
                    landed(dve, kv_in, a, ua, 16 * G)
                    at_least(dve, heads_summed, a)
                    nc.vector.tensor_tensor(kqe[:, :, :], kv[:, ua, :, 0:D],
                                            q_ps[ua % 2][:, 0:G * D].rearrange("p (g d) -> p g d", g=G), ALU.mult).then_inc(kq_done, 1)
                if messages:
                    at_least(dve, sums_ready, m - 1)
                    nc.vector.tensor_tensor(oh[:, um % 2, :, :], iota[:, 0:WIN].unsqueeze(1).to_broadcast((P, G, WIN)),
                                            rel[:, bass.ds(m * G, G)].unsqueeze(2).to_broadcast((P, G, WIN)),
                                            ALU.is_equal).then_inc(oh_built, 1)
                if scores:
                    dve.wait_ge(kq_done, a + 1)
                    dve.wait_ge(e_ready, a + 1)
                    nc.vector.tensor_tensor(kqe[:, :, :], kqe[:, :, :],
                                            e_ps[ua % 2][:, 0:G * D].rearrange("p (g d) -> p g d", g=G), ALU.mult).then_inc(kqe_done, 1)
                if messages:
                    dve.wait_ge(exp_done, m + 1)
                    nc.vector.tensor_tensor(msg[:, um % 2, :, 0:D].rearrange("p g (h d) -> p g h d", d=HD),
                                            kv[:, um, :, D:2 * D].rearrange("p g (h d) -> p g h d", d=HD),
                                            msg[:, um % 2, :, D:DZ].unsqueeze(3).to_broadcast((P, G, HEADS, HD)),
                                            ALU.mult).then_inc(msg_ready, 1)
                if scores:
                    dve.wait_ge(kqe_done, a + 1)
                    at_least(dve, score_ready, a)
                    nc.vector.tensor_reduce(raw_score[:, :], kqe[:, :, :].rearrange("p g (h d) -> p (g h) d", d=HD),
                                            AX_X, ALU.add).then_inc(heads_summed, 1)
                if sums:
                    if base is None:
                        base = dve.value_load(base_tab[0:1, bass.ds(n, 1)], min_val=0, max_val=N - 1)
                    if further:
                        further_sums(n, un, base)
                    dve.wait_ge(sums_ready, n + 1)
                    at_least(dve, acc_added, n)
                    acc = accT[0:DZ, bass.ds(base, WIN)]
                    nc.vector.tensor_tensor(acc, sum_ps[un % 2][0:DZ, 0:WIN], acc, ALU.add).then_inc(acc_added, 1)
                if scores:
                    dve.wait_ge(heads_summed, a + 1)
                    at_least(dve, exp_done, a - 1)
                    nc.vector.tensor_scalar(score[:, ua % 2, :], raw_score[:, :], -5.0, 5.0, ALU.max, ALU.min).then_inc(score_ready, 1)

            run_steps(dve, step, C, 4, lambda i: (load_most(dve, i), load_bases(dve, i * RING - 4)))

            out_batches = TILES // OUT_TILES

            def finish(b, h):
                dve.wait_ge(acc_turned, b + 1)
                sums = bank[h][0:NP, 0:OUT_TILES * DZ].rearrange("p (j f) -> p j f", f=DZ)
                zi, yb = z_inv[0:NP, h, :, :], y[0:NP, h, :, :]
                mean, var = stat[0:NP, h, 0, :], stat[0:NP, h, 1, :]
                nc.vector.tensor_scalar(zi, sums[:, :, D:DZ], 1e-6, None, ALU.add).then_inc(z_step, 1)
                dve.wait_ge(z_step, 2 * b + 1)
                nc.vector.reciprocal(zi, zi).then_inc(z_step, 1)
                dve.wait_ge(z_step, 2 * b + 2)
                nc.vector.tensor_tensor(yb.rearrange("p j (h d) -> p j h d", d=HD),
                                        sums[:, :, 0:D].rearrange("p j (h d) -> p j h d", d=HD),
                                        zi.unsqueeze(3).to_broadcast((NP, OUT_TILES, HEADS, HD)), ALU.mult).then_inc(y_attended, 1)
                dve.wait_ge(y_attended, b + 1)
                if isinstance(b, int):
                    dve.wait_ge(x_res_in[h], 32 * (b // 2 + 1))
                else:
                    dve.wait_ge(x_res_in[h], (b - h) * 16 + 32)
                nc.vector.tensor_tensor(yb, yb, x_res[0:NP, h, :, :], ALU.add).then_inc(y_step, 1)
                dve.wait_ge(y_step, 4 * b + 1)
                nc.vector.tensor_reduce(mean, yb, AX_X, ALU.add).then_inc(y_step, 1)
                dve.wait_ge(y_step, 4 * b + 2)
                nc.vector.tensor_scalar(mean, mean, 1.0 / D, None, ALU.mult).then_inc(y_step, 1)
                dve.wait_ge(y_step, 4 * b + 3)
                nc.vector.tensor_tensor(yb, yb, mean.unsqueeze(2).to_broadcast((NP, OUT_TILES, D)), ALU.subtract).then_inc(y_centred, 1)
                dve.wait_ge(squared, b + 1)
                nc.vector.tensor_reduce(var, ysq[0:NP, h, :, :], AX_X, ALU.add).then_inc(y_step, 1)
                dve.wait_ge(y_step, 4 * b + 4)
                nc.vector.tensor_scalar(stat[0:NP, h, 2, :], var, 1.0 / D, EPS_LN, ALU.mult, ALU.add).then_inc(var_ready, 1)
                dve.wait_ge(rooted, b + 1)
                nc.vector.reciprocal(stat[0:NP, h, 1, :], stat[0:NP, h, 3, :]).then_inc(std_inverted, 1)
                dve.wait_ge(std_inverted, b + 1)
                nc.vector.tensor_tensor(ysq[0:NP, h, :, :], yb,
                                        stat[0:NP, h, 1, :].unsqueeze(2).to_broadcast((NP, OUT_TILES, D)), ALU.mult).then_inc(y_ready, 1)

            with dve.Fori(0, out_batches // 2) as i:
                for h in range(2):
                    finish(i * 2 + h, h)
            finish(out_batches - 1, 0)


_INS = ['x', 'src', 'dst', 'edge_attr_96', 'L0_gnn_Wq', 'L0_gnn_bq', 'L0_gnn_Wk', 'L0_gnn_bk',
        'L0_gnn_We', 'L0_gnn_be', 'L0_gnn_Wv', 'L0_gnn_bv']


def kernel(**inputs):
    import numpy as _np
    import concourse.bacc as _bacc
    from concourse import mybir as _mybir
    from concourse.bass_utils import run_bass_kernel_spmd as _run

    nc = _bacc.Bacc("TRN2", target_bir_lowering=False, num_devices=1)
    arrays, args = {}, []
    for name in _INS:
        a = _np.ascontiguousarray(inputs[name])
        arrays[f"in_{name}_dram"] = a
        args.append(nc.dram_tensor(f"in_{name}_dram", a.shape, _mybir.dt.from_np(a.dtype), kind="ExternalInput").ap())
    args.append(nc.dram_tensor("out_0_dram", inputs["x"].shape, _mybir.dt.float32, kind="ExternalOutput").ap())
    gnn_kernel(nc, *args)
    r = _run(nc, [arrays], core_ids=[0])
    return r.results[0]["out_0_dram"]
```

```python
from contextlib import ExitStack

import concourse.bass as bass
from concourse import mybir

ALU = mybir.AluOpType
ACT = mybir.ActivationFunctionType
AX_X = mybir.AxisListType.X
F32 = mybir.dt.float32
BF16 = mybir.dt.bfloat16
I32 = mybir.dt.int32
I16 = mybir.dt.int16

P = 128
HEADS = 8
G = 4
CHUNK = P * G
WIN = 32
WIN_SHIFT = 5
PARTS = 3
SEL = WIN * PARTS
RING = 8
HALF = RING // 2
PAIR = 2
NP = 125
NP16 = 112
BATCH = 4
NOWHERE = -1.0e6


def at_least(engine, sem, value):
    if not (isinstance(value, int) and value <= 0):
        engine.wait_ge(sem, value)


def run_steps(engine, step, chunks, lag, round_values=None):
    rounds = (chunks - 1) // RING
    extra_args = () if round_values is None else (None, True)
    for s in range(RING):
        step(s, s, *extra_args)
    with engine.Fori(1, rounds) as i:
        if round_values is None:
            for u in range(RING):
                step(i * RING + u, u)
        else:
            most, values = round_values(i)
            with engine.If(most > 0):
                for u in range(RING):
                    step(i * RING + u, u, values[u], True)
            with engine.Else():
                for u in range(RING):
                    step(i * RING + u, u, values[u], False)
    for s in range(rounds * RING, chunks + lag):
        step(s, s % RING, *extra_args)


def run_batches(engine, step, batches, lag, shift=0, after_first=None, before_last=None):
    rounds = (batches - 1 - shift) // 4
    for b in range(4 + shift):
        step(b, b % 4)
    if after_first is not None:
        after_first()
    with engine.Fori(1, rounds) as i:
        for u in range(4):
            step(i * 4 + u + shift, (u + shift) % 4)
    if before_last is not None:
        before_last()
    for b in range(rounds * 4 + shift, batches + lag):
        step(b, b % 4)


def gnn_kernel(nc, x, src, dst, edge_attr, Wq, bq, Wk, bk, We, be, Wv, bv, out):
    N, D = x.shape
    E = src.shape[0]
    HD = D // HEADS
    DA = D + 1
    DZ = D + HEADS
    C = (E + CHUNK - 1) // CHUNK
    FULL = E // CHUNK
    DUP = C * CHUNK - E
    NQ = 115
    NJ = FULL // NQ
    ROUNDS = (C - 1) // RING
    TILES = N // NP
    N_PAD = (N + WIN + P - 1) // P * P
    QSCALE = float(HD) ** -0.5
    EPS_LN = 1e-5
    assert NQ * NJ == FULL and FULL == C - 1 and NP * TILES == N and DUP % G == 0
    BATCHES = TILES // BATCH
    assert C % PAIR == 0 and TILES % BATCH == 0 and BATCHES % 4 == 1 and 1 << WIN_SHIFT == WIN
    assert N_PAD < 1 << 15 and SEL <= P
    assert CHUNK <= 512 and BATCH * max(DZ, NP) <= 512 and NQ * G <= 512

    kv_dram = nc.dram_tensor("kv_table", (N, 2 * D), F32)
    q_dram = nc.dram_tensor("q_table", (N_PAD * PARTS, D), BF16)
    dst16_dram = nc.dram_tensor("dst_by_chunk", (C * CHUNK,), I16)
    base_dram = nc.dram_tensor("chunk_base", (C,), I32)
    extra_dram = nc.dram_tensor("chunk_extra_windows", (C,), I32)

    with ExitStack() as ctx:
        def sb(name, shape, dt=F32):
            return ctx.enter_context(nc.sbuf_tensor(name, shape, dt))

        def sem(name):
            return ctx.enter_context(nc.semaphore(name))

        iota_i = sb("iota_i", [P, P], I32)
        part_i = sb("part_i", [P, 1], I32)
        iota = sb("iota", [P, P])
        part = sb("part", [P, 1])
        sel_row_i = sb("sel_row_i", [P, 1], I32)
        sel_row = sb("sel_row", [P, 1])
        ident = sb("ident", [P, P])
        w_kvq = sb("w_kvq", [DA, 3 * D])
        w_e = sb("w_e", [DA, D])
        x_in = sb("x_in", [P, 4, BATCH, D])
        xT = sb("xT", [DA, 2, BATCH * NP])
        kv_out = sb("kv_out", [P, 4, BATCH, 2 * D])
        q_f = sb("q_f", [P, 4, BATCH, D])
        q_rest = sb("q_rest", [P, BATCH, D])
        q_out = sb("q_out", [P, 4, BATCH, PARTS, D], BF16)
        pad_rows = sb("pad_rows", [N_PAD - N, PARTS * D], BF16)
        accT = sb("accT", [P, N_PAD])
        dst_nat = accT[0:NQ, 0:NJ * CHUNK]
        dst16 = sb("dst16", [NQ, NJ * CHUNK], I16)
        dst16_end = sb("dst16_end", [1, CHUNK], I16)
        dst_end_row = sb("dst_end_row", [1, CHUNK], I32)
        dst_end = sb("dst_end", [P, G], I32)
        lohi = sb("lohi", [P, 4, NJ])
        lohi_i = sb("lohi_i", [P, 4, NJ], I32)
        lohi_end = sb("lohi_end", [1, 4])
        lohi_end_i = sb("lohi_end_i", [1, 4], I32)
        base_tab = sb("base_tab", [1, C], I32)
        extra_tab = sb("extra_tab", [1, C], I32)
        round_most = sb("round_most", [1, ROUNDS], I32)
        rounds_most = sb("rounds_most", [1, ROUNDS], I32)
        base_all = sb("base_all", [P, C], I32)
        minus_id = sb("minus_id", [SEL, C])
        rel = sb("rel", [P, C * G])
        ea = sb("ea", [P, RING, G, D])
        dst_b = sb("dst_b", [SEL, RING, CHUNK], I16)
        q_win = sb("q_win", [SEL, RING, D], BF16)
        src_idx = sb("src_idx", [P, RING, G], I32)
        kv = sb("kv", [P, RING, G, 2 * D])
        eaT = sb("eaT", [DA, 2, CHUNK])
        away = sb("away", [SEL, CHUNK], BF16)
        ohT = sb("ohT", [SEL, 2, CHUNK], BF16)
        oh = sb("oh", [P, 2, G, WIN])
        kqe = sb("kqe", [P, G, D])
        raw_score = sb("raw_score", [P, G * HEADS])
        score = sb("score", [P, 2, G * HEADS])
        msg = sb("msg", [P, 2, G, DZ])
        x_q_win = sb("x_q_win", [SEL, D], BF16)
        x_node_id = sb("x_node_id", [SEL, 1])
        x_ohT = sb("x_ohT", [SEL, CHUNK], BF16)
        x_rel = sb("x_rel", [P, G])
        x_oh = sb("x_oh", [P, G, WIN])
        accP = sb("accP", [DZ, 2, BATCH, NP])
        x_res = sb("x_res", [P, 4, BATCH, D])
        y = sb("y", [P, 4, BATCH, D])
        ysq = sb("ysq", [P, 2, BATCH, D])
        z_inv = sb("z_inv", [P, 2, BATCH, HEADS])
        y_sum = sb("y_sum", [P, 2, BATCH])
        minus_mean = sb("minus_mean", [P, 4, BATCH])
        sq_sum = sb("sq_sum", [P, 2, BATCH])
        var = sb("var", [P, 2, BATCH])
        std = sb("std", [P, 2, BATCH])
        std_inv = sb("std_inv", [P, 2, BATCH])
        shift = sb("shift", [P, 2, BATCH])

        bank = [ctx.enter_context(nc.psum_tensor(f"bank{i}", [P, 512], F32)) for i in range(8)]
        eaT_ps, e_ps, q_ps, sum_ps = bank[0:2], bank[2:4], bank[4:6], bank[6:8]

        iota_made = sem("iota_made")
        ident_step = sem("ident_step")
        ident_ready = sem("ident_ready")
        ones_ready = sem("ones_ready")
        w_kvq_in = sem("w_kvq_in")
        w_e_in = sem("w_e_in")
        dst_in = sem("dst_in")
        ends_in = sem("ends_in")
        pad_zeroed = sem("pad_zeroed")
        x_in_landed = [sem(f"x_in_landed{i}") for i in range(4)]
        x_turned = sem("x_turned")
        x_copied = sem("x_copied")
        kvq_done = sem("kvq_done")
        kv_evac = sem("kv_evac")
        q_evac = sem("q_evac")
        q_split = sem("q_split")
        q_parts_ready = sem("q_parts_ready")
        pad_stored = sem("pad_stored")
        tables_stored = [sem(f"tables_stored{i}") for i in range(4)]
        range_step = sem("range_step")
        range_ready = sem("range_ready")
        range_stored = sem("range_stored")
        dst_float = sem("dst_float")
        dst16_made = sem("dst16_made")
        dst16_stored = sem("dst16_stored")
        tabs_in = sem("tabs_in")
        node_id_ready = sem("node_id_ready")
        dst_turned = sem("dst_turned")
        rel_made = sem("rel_made")
        most_step = sem("most_step")
        most_ready = sem("most_ready")
        acc_zeroed = sem("acc_zeroed")
        ea_in = [sem(f"ea_in{i}") for i in range(RING)]
        dst_b_in = [sem(f"dst_b_in{i}") for i in range(2)]
        q_win_in = [sem(f"q_win_in{i}") for i in range(RING)]
        src_idx_in = [sem(f"src_idx_in{i}") for i in range(RING // PAIR)]
        loads_allowed = sem("loads_allowed")
        slots_taken = sem("slots_taken")
        kv_in = [sem(f"kv_in{i}") for i in range(RING)]
        ea_turned = sem("ea_turned")
        eaT_copied = sem("eaT_copied")
        e_ready = sem("e_ready")
        away_done = sem("away_done")
        ohT_built = sem("ohT_built")
        q_ready = sem("q_ready")
        kq_done = sem("kq_done")
        kqe_done = sem("kqe_done")
        heads_summed = sem("heads_summed")
        score_ready = sem("score_ready")
        exp_done = sem("exp_done")
        oh_built = sem("oh_built")
        msg_ready = sem("msg_ready")
        sums_ready = sem("sums_ready")
        acc_added = sem("acc_added")
        x_id_set = sem("x_id_set")
        x_load_go = sem("x_load_go")
        x_q_win_in = sem("x_q_win_in")
        x_ohT_built = sem("x_ohT_built")
        x_q_added = sem("x_q_added")
        x_rel_set = sem("x_rel_set")
        x_oh_built = sem("x_oh_built")
        x_sums_ready = sem("x_sums_ready")
        x_acc_added = sem("x_acc_added")
        accP_copied = sem("accP_copied")
        acc_turned = sem("acc_turned")
        x_res_in = [sem(f"x_res_in{i}") for i in range(4)]
        z_step = sem("z_step")
        y_attended = sem("y_attended")
        res_added = sem("res_added")
        y_summed = sem("y_summed")
        mean_ready = sem("mean_ready")
        squared = sem("squared")
        sq_summed = sem("sq_summed")
        var_ready = sem("var_ready")
        rooted = sem("rooted")
        std_inverted = sem("std_inverted")
        coef_ready = sem("coef_ready")
        y_ready = sem("y_ready")
        y_stored = [sem(f"y_stored{i}") for i in range(4)]

        kv_t = kv_dram.rearrange("(p t) d -> p t d", t=TILES)
        q_t = q_dram[0:N * PARTS, :].rearrange("(p t k) d -> p t k d", t=TILES, k=PARTS)
        x_t = x.rearrange("(p t) d -> p t d", t=TILES)
        out_t = out.rearrange("(p t) d -> p t d", t=TILES)
        NODE_PARTS = [(0, NP16), (NP16, NP)]

        def landed_half(engine, c, u):
            if isinstance(c, int):
                engine.wait_ge(dst_b_in[u // HALF], 16 * (c // RING + 1))
            else:
                engine.wait_ge(dst_b_in[u // HALF], (c - u) * (16 // RING) + 16)

        def landed(engine, sems, c, u, per_load):
            if isinstance(c, int):
                engine.wait_ge(sems[u], per_load * (c // RING + 1))
            else:
                engine.wait_ge(sems[u], (c - u) * (per_load // RING) + per_load)

        IN_TAB = "these tables hold a chunk's least destination and how many further windows it has"

        def load_bases(engine, first):
            return nc.values_load_multi_w_load_instructions(
                base_tab[0:1, bass.ds(first, RING)], engines=(engine.engine,), min_val=0, max_val=N - 1,
                skip_runtime_bounds_check_because=IN_TAB)[1]

        def load_most(engine, i):
            return nc.values_load_multi_w_load_instructions(
                rounds_most[0:1, bass.ds(i, 1)], engines=(engine.engine,), min_val=0, max_val=N // WIN,
                skip_runtime_bounds_check_because=IN_TAB)[1][0]

        def wait_tables(engine, b, u):
            engine.wait_ge(tables_stored[u], 48 * (b // 4 + 1) if isinstance(b, int) else (b - u) * 12 + 48)

        def wait_batch(engine, sems, b, u):
            engine.wait_ge(sems[u], 32 * (b // 4 + 1) if isinstance(b, int) else (b - u) * 8 + 32)

        def within(node):
            return nc.s_assert_within(node, 0, N - 1, skip_runtime_bounds_check_because=
                                      "a chunk's windows end with the one that holds its greatest destination")

        block = ctx.enter_context(nc.Block())

        @block.sync
        def _(sp):
            def load_x(b, h):
                for lo, hi in NODE_PARTS:
                    sp.dma_start(x_in[lo:hi, h, :, :], x_t[lo:hi, bass.ds(b * BATCH, BATCH), :]).then_inc(x_in_landed[h], 16)

            def load_sources(s, u):
                q = u // PAIR
                count = min(PAIR, C - s) if isinstance(s, int) else PAIR
                whole = count - 1 if isinstance(s, int) and s + count == C else count
                sp.dma_start(src_idx[:, u:u + whole, :], src[bass.ds(s * CHUNK, whole * CHUNK)].rearrange(
                    "(c p g) -> p c g", p=P, g=G)).then_inc(src_idx_in[q], 16)
                if whole < count:
                    sp.dma_start(src_idx[:, u + whole, :], src[E - CHUNK:E].rearrange(
                        "(p g) -> p g", g=G)).then_inc(src_idx_in[q], 16)

            def node_batch(b, u):
                if not isinstance(b, int) or b + 3 < BATCHES:
                    at_least(sp, x_turned, b)
                    load_x(b + 3, (u + 3) % 4)
                if not isinstance(b, int) or b >= 1:
                    m, um = b - 1, (u - 1) % 4
                    sp.wait_ge(kv_evac, b * BATCH)
                    sp.wait_ge(q_parts_ready, b)
                    for lo, hi in NODE_PARTS:
                        sp.dma_start(kv_t[lo:hi, bass.ds(m * BATCH, BATCH), :], kv_out[lo:hi, um, :, :]).then_inc(tables_stored[um], 16)
                    sp.dma_start(q_t[:, bass.ds(m * BATCH, BATCH), :, :], q_out[0:NP, um, :, :, :]).then_inc(tables_stored[um], 16)

            for b in range(3):
                load_x(b, b)
            sp.dma_start(dst_nat.bitcast(I32), dst[0:FULL * CHUNK].rearrange("(q r) -> q r", q=NQ)).then_inc(dst_in, 16)
            sp.dma_start(dst_end_row[:, :], dst[E - CHUNK:E].rearrange("(a r) -> a r", a=1)).then_inc(ends_in, 16)
            sp.dma_start(dst_end[:, :], dst[E - CHUNK:E].rearrange("(p g) -> p g", g=G)).then_inc(ends_in, 16)
            sp.wait_ge(pad_zeroed, 1)
            sp.dma_start(q_dram[N * PARTS:N_PAD * PARTS, :].rearrange("(n k) d -> n (k d)", k=PARTS), pad_rows[:, :]).then_inc(pad_stored, 16)
            for c in range(0, RING, PAIR):
                load_sources(c, c)
            run_batches(sp, node_batch, BATCHES, 1, 1)

            sp.wait_ge(dst16_made, 2)
            sp.dma_start(dst16_dram[0:FULL * CHUNK].rearrange("(q r) -> q r", q=NQ), dst16[:, :]).then_inc(dst16_stored, 16)
            sp.dma_start(dst16_dram[FULL * CHUNK:C * CHUNK].rearrange("(a r) -> a r", a=1), dst16_end[:, :]).then_inc(dst16_stored, 16)

            sp.wait_ge(range_ready, 1)
            sp.dma_start(base_dram[0:FULL].rearrange("(q j) -> q j", j=NJ), lohi_i[0:NQ, 0, :]).then_inc(range_stored, 16)
            sp.dma_start(extra_dram[0:FULL].rearrange("(q j) -> q j", j=NJ), lohi_i[0:NQ, 3, :]).then_inc(range_stored, 16)
            sp.dma_start(base_dram[FULL:C].rearrange("(a r) -> a r", a=1), lohi_end_i[:, 0:1]).then_inc(range_stored, 16)
            sp.dma_start(extra_dram[FULL:C].rearrange("(a r) -> a r", a=1), lohi_end_i[:, 3:4]).then_inc(range_stored, 16)
            sp.wait_ge(range_stored, 64)
            sp.dma_start(base_tab[:, :], base_dram.rearrange("(a c) -> a c", a=1)).then_inc(tabs_in, 16)
            sp.dma_start(extra_tab[:, :], extra_dram.rearrange("(a c) -> a c", a=1)).then_inc(tabs_in, 16)
            sp.dma_start(base_all[:, :], base_dram.rearrange("(a c) -> a c", a=1).to_broadcast((P, C))).then_inc(tabs_in, 16)
            sp.wait_ge(dst16_stored, 32)
            sp.wait_ge(tabs_in, 48)
            sp.wait_ge(most_ready, 1)
            sp.wait_ge(pad_stored, 16)
            for u in range(4):
                sp.wait_ge(tables_stored[u], 48 * ((BATCHES - u + 3) // 4))

            def load_destinations(s, h):
                count = min(HALF, C - s) if isinstance(s, int) else HALF
                sp.dma_start(dst_b[:, h * HALF:h * HALF + count, :], dst16_dram[bass.ds(s * CHUNK, count * CHUNK)].rearrange(
                    "(a c r) -> a c r", a=1, c=count).to_broadcast((SEL, count, CHUNK))).then_inc(dst_b_in[h], 16)

            def step(s, u, base, further):
                if not isinstance(s, int) or s < C:
                    first_edge = (E - CHUNK if s == C - 1 else s * CHUNK) if isinstance(s, int) else s * CHUNK
                    if base is None:
                        base = sp.value_load(base_tab[0:1, bass.ds(s, 1)], min_val=0, max_val=N - 1)
                    if u % PAIR == 0 and (not isinstance(s, int) or s >= RING):
                        sp.wait_ge(kq_done, s - RING + PAIR)
                        sp.sem_inc(loads_allowed, 1)
                        load_sources(s, u)
                    used = s - (HALF if u % HALF == 0 else RING - 1)
                    at_least(sp, ea_turned, used)
                    at_least(sp, kq_done, used)
                    if u % PAIR == 0:
                        sp.sem_inc(loads_allowed, 1)
                    if u % HALF == 0:
                        load_destinations(s, u // HALF)
                    sp.dma_start(ea[:, u, :, :], edge_attr[bass.ds(first_edge, CHUNK), :].rearrange(
                        "(p g) d -> p g d", g=G)).then_inc(ea_in[u], 16)
                    sp.dma_start(q_win[:, u, :], q_dram[bass.ds(base * PARTS, SEL), :]).then_inc(q_win_in[u], 16)
                if not further:
                    return
                c = s - 3
                if isinstance(s, int) and not 0 <= c < C:
                    return
                extra = sp.value_load(extra_tab[0:1, bass.ds(c, 1)], min_val=0, max_val=N // WIN)
                with sp.If(extra > 0):
                    base = sp.value_load(base_tab[0:1, bass.ds(c, 1)], min_val=0, max_val=N - 1)
                    with sp.Fori(0, extra) as j:
                        sp.wait_ge(x_load_go, 1)
                        sp.sem_clear(x_load_go)
                        row = within(base + (j + 1) * WIN)
                        sp.dma_start(x_q_win[:, :], q_dram[bass.ds(row * PARTS, SEL), :]).then_inc(x_q_win_in, 16)

            run_steps(sp, step, C, 3, lambda i: (load_most(sp, i), load_bases(sp, i * RING)))

            def load_res(b, u):
                for lo, hi in NODE_PARTS:
                    sp.dma_start(x_res[lo:hi, u, :, :], x_t[lo:hi, bass.ds(b * BATCH, BATCH), :]).then_inc(x_res_in[u], 16)

            def output(b, u):
                if not isinstance(b, int) or b + 1 < BATCHES:
                    at_least(sp, res_added, b - 2)
                    load_res(b + 1, (u + 1) % 4)
                if not isinstance(b, int) or b >= 2:
                    v = (u - 2) % 4
                    sp.wait_ge(y_ready, b - 1)
                    for lo, hi in NODE_PARTS:
                        sp.dma_start(out_t[lo:hi, bass.ds((b - 2) * BATCH, BATCH), :], y[lo:hi, v, :, :]).then_inc(y_stored[v], 16)

            load_res(0, 0)
            run_batches(sp, output, BATCHES, 2)
            for u in range(4):
                sp.wait_ge(y_stored[u], 32 * ((BATCHES - u + 3) // 4))

        @block.gpsimd
        def _(pool):
            nc.gpsimd.iota(iota_i[:, :], pattern=[[1, P]], base=0, channel_multiplier=0).then_inc(iota_made, 1)
            nc.gpsimd.iota(part_i[:, :], pattern=[[0, 1]], base=0, channel_multiplier=1).then_inc(iota_made, 1)
            pool.wait_ge(iota_made, 2)
            nc.gpsimd.iota(sel_row_i[:, :], pattern=[[0, 1]], base=0,
                           channel_multiplier=(512 + PARTS - 1) // PARTS).then_inc(iota_made, 1)
            pool.wait_ge(iota_made, 3)
            nc.gpsimd.memset(xT[D:DA, :, :], 1.0).then_inc(ones_ready, 1)
            pool.wait_ge(ones_ready, 1)
            nc.gpsimd.memset(eaT[D:DA, :, :], 1.0).then_inc(ones_ready, 1)
            pool.wait_ge(ones_ready, 2)
            nc.gpsimd.memset(pad_rows[:, :], 0.0).then_inc(pad_zeroed, 1)
            pool.wait_ge(pad_zeroed, 1)
            nc.gpsimd.memset(accT[:, NJ * CHUNK:N_PAD], 0.0).then_inc(acc_zeroed, 1)

            pool.wait_ge(acc_zeroed, 1)
            pool.wait_ge(dst_in, 16)
            nc.gpsimd.tensor_copy(dst_nat, dst_nat.bitcast(I32)).then_inc(dst_float, 1)
            pool.wait_ge(dst_float, 1)
            nc.gpsimd.tensor_copy(dst16[:, :], dst_nat).then_inc(dst16_made, 1)
            pool.wait_ge(dst16_made, 1)
            pool.wait_ge(ends_in, 32)
            nc.gpsimd.tensor_copy(dst16_end[:, :], dst_end_row[:, :]).then_inc(dst16_made, 1)

            for u in range(4):
                pool.wait_ge(tables_stored[u], 48 * ((BATCHES - u + 3) // 4))

            def step(s, u):
                at_least(pool, msg_ready, s - RING + 1)
                if u % PAIR == 0:
                    if isinstance(s, int):
                        pool.wait_ge(src_idx_in[u // PAIR], 16 * (s // RING + 1 + (s + PAIR == C)))
                    else:
                        pool.wait_ge(src_idx_in[u // PAIR], (s - u) * (16 // RING) + 16)
                pool.sem_inc(slots_taken, 1)
                for g in range(G):
                    pool.indirect_dma_start(kv[:, u, g, :], None, kv_dram[:, :],
                                            bass.IndirectOffsetOnAxis(ap=src_idx[:, u, g:g + 1], axis=0)
                                            ).then_inc(kv_in[u], 16)

            run_steps(pool, step, C, 0)

        @block.tensor
        def _(pe):
            pe.wait_ge(ident_ready, 1)


            def node_batch(b, u):
                h = u % 2
                if not isinstance(b, int) or b < BATCHES:
                    wait_batch(pe, x_in_landed, b, u)
                    at_least(pe, x_copied, b - 1)
                    for j in range(BATCH):
                        last = nc.tensor.transpose(bank[h][0:D, j * NP:(j + 1) * NP], x_in[0:NP, u, j, :],
                                                   ident[0:NP, 0:NP])
                    last.then_inc(x_turned, 1)
                if not isinstance(b, int) or b >= 1:
                    if isinstance(b, int) and b == 1:
                        pe.wait_ge(ones_ready, 1)
                        pe.wait_ge(w_kvq_in, 16 * 6)
                    pe.wait_ge(x_copied, b)
                    for j in range(BATCH):
                        t = (b - 1) * BATCH + j
                        at_least(pe, q_evac, t - BATCH + 1)
                        nc.tensor.matmul(bank[2 + j][0:NP, 0:3 * D], xT[:, 1 - h, j * NP:(j + 1) * NP], w_kvq[:, :],
                                         start=True, stop=True).then_inc(kvq_done, 1)

            run_batches(pe, node_batch, BATCHES, 1, 1)

            pe.wait_ge(dst_float, 1)
            for j in range(NJ):
                at_least(pe, rel_made, j - 1)
                rows = dst_nat[:, j * CHUNK:(j + 1) * CHUNK].rearrange("q (p g) -> q g p", g=G)
                for g in range(G):
                    last = nc.tensor.transpose(bank[6 + j % 2][:, g * NQ:(g + 1) * NQ], rows[:, g, :], ident[0:NQ, 0:NQ])
                last.then_inc(dst_turned, 1)

            pe.wait_ge(q_evac, TILES)
            pe.wait_ge(rel_made, NJ + 1)
            pe.wait_ge(most_ready, 1)
            pe.wait_ge(w_e_in, 32)
            pe.wait_ge(ones_ready, 2)

            def step(s, u, _, further):
                c, v = s - 1, (u - 1) % RING
                turning = not isinstance(s, int) or s < C
                projecting = not isinstance(s, int) or 0 <= c < C
                if turning:
                    landed(pe, ea_in, s, u, 16)
                if projecting:
                    pe.wait_ge(eaT_copied, c + 1)
                    at_least(pe, kqe_done, c - 1)
                for g in range(G):
                    if turning:
                        turned = nc.tensor.transpose(eaT_ps[u % 2][0:D, g * P:(g + 1) * P], ea[:, u, g, :], ident[:, :])
                    if projecting:
                        projected = nc.tensor.matmul(e_ps[v % 2][:, g * D:(g + 1) * D], eaT[:, v % 2, g * P:(g + 1) * P],
                                                     w_e[:, :], start=True, stop=True)
                if turning:
                    turned.then_inc(ea_turned, 1)
                if projecting:
                    projected.then_inc(e_ready, 1)
                    pe.wait_ge(ohT_built, c + 1)
                    landed(pe, q_win_in, c, v, 16)
                    sel = ohT[:, v % 2, :].rearrange("n (p g) -> n g p", g=G)
                    for g in range(G):
                        last = nc.tensor.matmul(q_ps[v % 2][:, g * D:(g + 1) * D], sel[:, g, :], q_win[:, v, :],
                                                start=(g == 0), stop=(g == G - 1), skip_group_check=True)
                    last.then_inc(q_ready, 1)
                    if further:
                        extra = pe.value_load(extra_tab[0:1, bass.ds(c, 1)], min_val=0, max_val=N // WIN)
                        with pe.If(extra > 0):
                            x_sel = x_ohT[:, :].rearrange("n (p g) -> n g p", g=G)
                            with pe.Fori(0, extra) as j:
                                pe.wait_ge(x_ohT_built, 1)
                                pe.sem_clear(x_ohT_built)
                                pe.wait_ge(x_q_win_in, 16)
                                pe.sem_clear(x_q_win_in)
                                for g in range(G):
                                    last = nc.tensor.matmul(q_ps[v % 2][:, g * D:(g + 1) * D], x_sel[:, g, :], x_q_win[:, :],
                                                            start=False, stop=(g == G - 1), skip_group_check=True)
                                last.then_inc(x_q_added, 1)
                c, v = s - 3, (u - 3) % RING
                if not isinstance(s, int) or 0 <= c < C:
                    if further:
                        extra = pe.value_load(extra_tab[0:1, bass.ds(c, 1)], min_val=0, max_val=N // WIN)
                        with pe.If(extra > 0):
                            with pe.Fori(0, extra) as j:
                                pe.wait_ge(x_oh_built, 1)
                                pe.sem_clear(x_oh_built)
                                pe.wait_ge(msg_ready, c + 1)
                                at_least(pe, acc_added, c - 1)
                                for g in range(G):
                                    last = nc.tensor.matmul(sum_ps[v % 2][0:DZ, 0:WIN], msg[:, v % 2, g, :], x_oh[:, g, :],
                                                            start=(g == 0), stop=(g == G - 1))
                                last.then_inc(x_sums_ready, 1)
                                pe.wait_ge(x_acc_added, 1)
                                pe.sem_clear(x_acc_added)
                    pe.wait_ge(msg_ready, c + 1)
                    pe.wait_ge(oh_built, c + 1)
                    at_least(pe, acc_added, c - 1)
                    for g in range(G):
                        last = nc.tensor.matmul(sum_ps[v % 2][0:DZ, 0:WIN], msg[:, v % 2, g, :], oh[:, v % 2, g, :],
                                                start=(g == 0), stop=(g == G - 1))
                    last.then_inc(sums_ready, 1)

            run_steps(pe, step, C, 3, lambda i: (load_most(pe, i), [None] * RING))

            def turn_back(b, u):
                h = u % 2
                pe.wait_ge(accP_copied, b + 1)
                at_least(pe, y_attended, b - 1)
                for j in range(BATCH):
                    last = nc.tensor.transpose(bank[h][0:NP, j * DZ:(j + 1) * DZ], accP[:, h, j, :], ident[0:DZ, 0:DZ])
                last.then_inc(acc_turned, 1)

            run_batches(pe, turn_back, BATCHES, 0)

        @block.scalar
        def _(act):
            for k, (w, b) in enumerate(((Wk, bk), (Wv, bv), (Wq, bq))):
                act.dma_start(w_kvq[0:D, k * D:(k + 1) * D], w[:, :]).then_inc(w_kvq_in, 16)
                act.dma_start(w_kvq[D:DA, k * D:(k + 1) * D],
                              b.rearrange("(a d) -> a d", a=1)).then_inc(w_kvq_in, 16)
            act.dma_start(w_e[0:D, :], We[:, :]).then_inc(w_e_in, 16)
            act.dma_start(w_e[D:DA, :], be.rearrange("(a d) -> a d", a=1)).then_inc(w_e_in, 16)

            def node_batch(b, u):
                h = u % 2
                if not isinstance(b, int) or b < BATCHES:
                    act.wait_ge(x_turned, b + 1)
                    at_least(act, kvq_done, (b - 1) * BATCH)
                    nc.scalar.copy(xT[0:D, h, :], bank[h][0:D, 0:BATCH * NP]).then_inc(x_copied, 1)
                if not isinstance(b, int) or b >= 1:
                    m, um = b - 1, (u - 1) % 4
                    if not isinstance(b, int) or m >= 4:
                        wait_tables(act, m - 4, um)
                    at_least(act, q_parts_ready, m - 3)
                    for j in range(BATCH):
                        act.wait_ge(kvq_done, m * BATCH + j + 1)
                        nc.scalar.copy(kv_out[0:NP, um, j, :], bank[2 + j][0:NP, 0:2 * D]).then_inc(kv_evac, 1)
                        nc.scalar.activation(q_f[0:NP, um, j, :], bank[2 + j][0:NP, 2 * D:3 * D], ACT.Copy,
                                             scale=QSCALE).then_inc(q_evac, 1)

            run_batches(act, node_batch, BATCHES, 1, 1)

            act.wait_ge(node_id_ready, 1)

            def step(s, u):
                if not isinstance(s, int) or s < C:
                    act.wait_ge(ea_turned, s + 1)
                    at_least(act, e_ready, s - 1)
                    nc.scalar.copy(eaT[0:D, u % 2, :], eaT_ps[u % 2][0:D, :]).then_inc(eaT_copied, 1)
                    if u % HALF == 0:
                        landed_half(act, s, u)
                    at_least(act, ohT_built, s)
                    nc.scalar.activation(away[:, :], dst_b[:, u, :], ACT.Abs,
                                         bias=minus_id[:, bass.ds(s, 1)]).then_inc(away_done, 1)
                    act.wait_ge(away_done, s + 1)
                    at_least(act, q_ready, s - 1)
                    nc.scalar.activation(ohT[:, u % 2, :], away[:, :], ACT.Relu, bias=1.0, scale=-1.0).then_inc(ohT_built, 1)
                c, v = s - 2, (u - 2) % RING
                if not isinstance(s, int) or 0 <= c < C:
                    act.wait_ge(score_ready, c + 1)
                    at_least(act, acc_added, c - 1)
                    nc.scalar.activation(msg[:, v % 2, :, D:DZ],
                                         score[:, v % 2, :].rearrange("p (g h) -> p g h", g=G), ACT.Exp).then_inc(exp_done, 1)

            run_steps(act, step, C, 2)

            acc_cols = accT[0:DZ, 0:N].rearrange("f (p t) -> f t p", t=TILES)
            act.wait_ge(acc_added, C)

            def collect(b, h):
                at_least(act, acc_turned, b - 1)
                nc.scalar.copy(accP[:, h, :, :], acc_cols[:, bass.ds(b * BATCH, BATCH), :]).then_inc(accP_copied, 1)

            def output(b, u):
                if not isinstance(b, int) or b + 1 < BATCHES:
                    collect(b + 1, (u + 1) % 2)
                if not isinstance(b, int) or b >= 2:
                    v = (u - 2) % 4
                    act.wait_ge(coef_ready, b - 1)
                    for j in range(BATCH):
                        last = nc.scalar.activation(y[0:NP, v, j, :], y[0:NP, v, j, :], ACT.Identity,
                                                    scale=std_inv[0:NP, v % 2, j:j + 1], bias=shift[0:NP, v % 2, j:j + 1])
                    last.then_inc(y_ready, 1)
                if not isinstance(b, int) or 1 <= b <= BATCHES:
                    v = (u - 1) % 4
                    act.wait_ge(var_ready, b)
                    at_least(act, std_inverted, b - 2)
                    nc.scalar.activation(std[0:NP, v % 2, :], var[0:NP, v % 2, :], ACT.Sqrt).then_inc(rooted, 1)
                if not isinstance(b, int) or b < BATCHES:
                    act.wait_ge(mean_ready, b + 1)
                    at_least(act, sq_summed, b - 1)
                    for j in range(BATCH):
                        last = nc.scalar.activation(ysq[0:NP, u % 2, j, :], y[0:NP, u, j, :], ACT.Square,
                                                    bias=minus_mean[0:NP, u, j:j + 1])
                    last.then_inc(squared, 1)

            collect(0, 0)
            run_batches(act, output, BATCHES, 2)

        @block.vector
        def _(dve):
            dve.wait_ge(iota_made, 3)
            nc.vector.tensor_copy(iota[:, :], iota_i[:, :]).then_inc(ident_step, 1)
            nc.vector.tensor_copy(part[:, :], part_i[:, :]).then_inc(ident_step, 1)
            nc.vector.tensor_scalar(sel_row_i[:, :], sel_row_i[:, :], 9, None, ALU.logical_shift_right).then_inc(ident_step, 1)
            dve.wait_ge(ident_step, 3)
            nc.vector.tensor_copy(sel_row[:, :], sel_row_i[:, :]).then_inc(ident_step, 1)
            nc.vector.tensor_tensor(ident[:, :], iota[:, :], part[:, 0:1].to_broadcast((P, P)), ALU.is_equal).then_inc(ident_ready, 1)

            def node_batch(b, u):
                q, rest = q_f[0:NP, u, :, :], q_rest[0:NP, :, :]
                parts = [q_out[0:NP, u, :, i, :] for i in range(PARTS)]
                dve.wait_ge(q_evac, (b + 1) * BATCH)
                if not isinstance(b, int) or b >= 4:
                    wait_tables(dve, b - 4, u)
                nc.vector.tensor_copy(parts[0], q).then_inc(q_split, 1)
                dve.wait_ge(q_split, b * 3 + 1)
                at_least(dve, q_parts_ready, b)
                nc.vector.tensor_tensor(rest, q, parts[0], ALU.subtract).then_inc(q_split, 1)
                dve.wait_ge(q_split, b * 3 + 2)
                nc.vector.tensor_copy(parts[1], rest).then_inc(q_split, 1)
                dve.wait_ge(q_split, b * 3 + 3)
                nc.vector.tensor_tensor(parts[2], rest, parts[1], ALU.subtract).then_inc(q_parts_ready, 1)

            rows = dst_nat.rearrange("q (j r) -> q j r", j=NJ)

            def least():
                dve.wait_ge(dst_float, 1)
                nc.vector.tensor_reduce(lohi[0:NQ, 0, :], rows, AX_X, ALU.min).then_inc(range_step, 1)

            def greatest():
                nc.vector.tensor_reduce(lohi[0:NQ, 1, :], rows, AX_X, ALU.max).then_inc(range_step, 1)

            run_batches(dve, node_batch, BATCHES, 0, 1, least, greatest)

            dve.wait_ge(ends_in, 32)
            nc.vector.tensor_reduce(lohi_end[:, 0:1], dst_end_row[:, :], AX_X, ALU.min).then_inc(range_step, 1)
            nc.vector.tensor_reduce(lohi_end[:, 1:2], dst_end_row[:, :], AX_X, ALU.max).then_inc(range_step, 1)
            dve.wait_ge(range_step, 4)
            nc.vector.tensor_copy(lohi_i[0:NQ, 0, :], lohi[0:NQ, 0, :]).then_inc(range_step, 1)
            nc.vector.tensor_tensor(lohi_i[0:NQ, 2, :], lohi[0:NQ, 1, :], lohi[0:NQ, 0, :], ALU.subtract).then_inc(range_step, 1)
            nc.vector.tensor_copy(lohi_end_i[:, 0:1], lohi_end[:, 0:1]).then_inc(range_step, 1)
            nc.vector.tensor_tensor(lohi_end_i[:, 2:3], lohi_end[:, 1:2], lohi_end[:, 0:1], ALU.subtract).then_inc(range_step, 1)
            dve.wait_ge(range_step, 8)
            nc.vector.tensor_scalar(lohi_i[0:NQ, 3, :], lohi_i[0:NQ, 2, :], WIN_SHIFT, None, ALU.logical_shift_right).then_inc(range_step, 1)
            dve.wait_ge(range_step, 9)
            nc.vector.tensor_scalar(lohi_end_i[:, 3:4], lohi_end_i[:, 2:3], WIN_SHIFT, None, ALU.logical_shift_right).then_inc(range_ready, 1)

            rel_v = rel[:, 0:FULL * G].rearrange("p (q j g) -> p q j g", j=NJ, g=G)
            for j in range(NJ):
                dve.wait_ge(dst_turned, j + 1)
                ps = bank[6 + j % 2][:, 0:G * NQ].rearrange("p (g q) -> p q g", g=G)
                nc.vector.tensor_copy(rel_v[:, :, j, :], ps).then_inc(rel_made, 1)
            nc.vector.tensor_copy(rel[:, FULL * G:C * G], dst_end[:, :]).then_inc(rel_made, 1)
            dve.wait_ge(tabs_in, 48)
            nc.vector.tensor_reduce(round_most[:, :], extra_tab[:, 0:ROUNDS * RING].rearrange("a (i c) -> a i c", c=RING),
                                    AX_X, ALU.max).then_inc(most_step, 1)
            dve.wait_ge(most_step, 1)
            nc.vector.tensor_tensor(rounds_most[:, 1:ROUNDS], round_most[:, 0:ROUNDS - 1], round_most[:, 1:ROUNDS],
                                    ALU.max).then_inc(most_ready, 1)
            dve.wait_ge(most_ready, 1)
            dve.wait_ge(rel_made, NJ + 1)
            nc.vector.tensor_scalar(minus_id[:, :], base_all[0:SEL, :], sel_row[0:SEL, 0:1], -1.0,
                                    ALU.add, ALU.mult).then_inc(node_id_ready, 1)
            rel_cg = rel[:, :].rearrange("p (c g) -> p c g", g=G)
            nc.vector.tensor_tensor(rel_cg, rel_cg, base_all[:, :].unsqueeze(2).to_broadcast((P, C, G)),
                                    ALU.subtract).then_inc(node_id_ready, 1)
            dve.wait_ge(node_id_ready, 2)
            nc.vector.memset(rel[0:DUP // G, FULL * G:C * G], NOWHERE).then_inc(node_id_ready, 1)
            dve.wait_ge(node_id_ready, 3)
            dve.wait_ge(dst16_made, 1)
            nc.vector.memset(accT[:, 0:NJ * CHUNK], 0.0).then_inc(acc_zeroed, 1)
            dve.wait_ge(acc_zeroed, 2)

            def further_q(c, v):
                extra = dve.value_load(extra_tab[0:1, bass.ds(c, 1)], min_val=0, max_val=N // WIN)
                with dve.If(extra > 0):
                    nc.vector.tensor_scalar(x_node_id[:, :], minus_id[:, bass.ds(c, 1)], -1.0, None, ALU.mult).then_inc(x_id_set, 1)
                    dve.wait_ge(x_id_set, 1)
                    dve.sem_clear(x_id_set)
                    with dve.Fori(0, extra) as j:
                        dve.sem_inc(x_load_go, 1)
                        nc.vector.tensor_scalar(x_node_id[:, :], x_node_id[:, :], float(WIN), None, ALU.add).then_inc(x_id_set, 1)
                        dve.wait_ge(x_id_set, 1)
                        dve.sem_clear(x_id_set)
                        nc.vector.tensor_tensor(x_ohT[:, :], dst_b[:, v, :], x_node_id[:, 0:1].to_broadcast((SEL, CHUNK)),
                                                ALU.is_equal).then_inc(x_ohT_built, 1)
                        dve.wait_ge(x_q_added, 1)
                        dve.sem_clear(x_q_added)

            def further_sums(c, v, base):
                extra = dve.value_load(extra_tab[0:1, bass.ds(c, 1)], min_val=0, max_val=N // WIN)
                with dve.If(extra > 0):
                    nc.vector.tensor_copy(x_rel[:, :], rel[:, bass.ds(c * G, G)]).then_inc(x_rel_set, 1)
                    dve.wait_ge(x_rel_set, 1)
                    dve.sem_clear(x_rel_set)
                    with dve.Fori(0, extra) as j:
                        nc.vector.tensor_scalar(x_rel[:, :], x_rel[:, :], float(-WIN), None, ALU.add).then_inc(x_rel_set, 1)
                        dve.wait_ge(x_rel_set, 1)
                        dve.sem_clear(x_rel_set)
                        nc.vector.tensor_tensor(x_oh[:, :, :], iota[:, 0:WIN].unsqueeze(1).to_broadcast((P, G, WIN)),
                                                x_rel[:, :].unsqueeze(2).to_broadcast((P, G, WIN)),
                                                ALU.is_equal).then_inc(x_oh_built, 1)
                        dve.wait_ge(x_sums_ready, 1)
                        dve.sem_clear(x_sums_ready)
                        at_least(dve, acc_added, c)
                        col = within(base + (j + 1) * WIN)
                        acc = accT[0:DZ, bass.ds(col, WIN)]
                        nc.vector.tensor_tensor(acc, sum_ps[v % 2][0:DZ, 0:WIN], acc, ALU.add).then_inc(x_acc_added, 1)

            def step(s, u, base, further):
                a, m, n = s - 2, s - 3, s - 4
                ua, um, un = (u - 2) % RING, (u - 3) % RING, (u - 4) % RING
                scores = not isinstance(s, int) or 0 <= a < C
                messages = not isinstance(s, int) or 0 <= m < C
                sums = not isinstance(s, int) or 0 <= n < C
                if scores:
                    dve.wait_ge(q_ready, a + 1)
                    if further:
                        further_q(a, ua)
                    landed(dve, kv_in, a, ua, 16 * G)
                    at_least(dve, heads_summed, a)
                    nc.vector.tensor_tensor(kqe[:, :, :], kv[:, ua, :, 0:D],
                                            q_ps[ua % 2][:, 0:G * D].rearrange("p (g d) -> p g d", g=G), ALU.mult).then_inc(kq_done, 1)
                if messages:
                    at_least(dve, sums_ready, m - 1)
                    nc.vector.tensor_tensor(oh[:, um % 2, :, :], iota[:, 0:WIN].unsqueeze(1).to_broadcast((P, G, WIN)),
                                            rel[:, bass.ds(m * G, G)].unsqueeze(2).to_broadcast((P, G, WIN)),
                                            ALU.is_equal).then_inc(oh_built, 1)
                if scores:
                    dve.wait_ge(kq_done, a + 1)
                    dve.wait_ge(e_ready, a + 1)
                    nc.vector.tensor_tensor(kqe[:, :, :], kqe[:, :, :],
                                            e_ps[ua % 2][:, 0:G * D].rearrange("p (g d) -> p g d", g=G), ALU.mult).then_inc(kqe_done, 1)
                if messages:
                    dve.wait_ge(exp_done, m + 1)
                    nc.vector.tensor_tensor(msg[:, um % 2, :, 0:D].rearrange("p g (h d) -> p g h d", d=HD),
                                            kv[:, um, :, D:2 * D].rearrange("p g (h d) -> p g h d", d=HD),
                                            msg[:, um % 2, :, D:DZ].unsqueeze(3).to_broadcast((P, G, HEADS, HD)),
                                            ALU.mult).then_inc(msg_ready, 1)
                if scores:
                    dve.wait_ge(kqe_done, a + 1)
                    at_least(dve, score_ready, a)
                    nc.vector.tensor_reduce(raw_score[:, :], kqe[:, :, :].rearrange("p g (h d) -> p (g h) d", d=HD),
                                            AX_X, ALU.add).then_inc(heads_summed, 1)
                if sums:
                    if base is None:
                        base = dve.value_load(base_tab[0:1, bass.ds(n, 1)], min_val=0, max_val=N - 1)
                    if further:
                        further_sums(n, un, base)
                    dve.wait_ge(sums_ready, n + 1)
                    at_least(dve, acc_added, n)
                    acc = accT[0:DZ, bass.ds(base, WIN)]
                    nc.vector.tensor_tensor(acc, sum_ps[un % 2][0:DZ, 0:WIN], acc, ALU.add).then_inc(acc_added, 1)
                if scores:
                    dve.wait_ge(heads_summed, a + 1)
                    at_least(dve, exp_done, a - 1)
                    nc.vector.tensor_scalar(score[:, ua % 2, :], raw_score[:, :], -5.0, 5.0, ALU.max, ALU.min).then_inc(score_ready, 1)

            run_steps(dve, step, C, 4, lambda i: (load_most(dve, i), load_bases(dve, i * RING - 4)))

            def output(b, u):
                h, v, w = u % 2, (u - 1) % 4, (u - 2) % 4
                first = not isinstance(b, int) or b < BATCHES
                second = not isinstance(b, int) or 1 <= b <= BATCHES
                third = not isinstance(b, int) or b >= 2
                sums = bank[h][0:NP, 0:BATCH * DZ].rearrange("p (j f) -> p j f", f=DZ)
                zi, yb = z_inv[0:NP, h, :, :], y[0:NP, u, :, :]
                if first:
                    dve.wait_ge(acc_turned, b + 1)
                    nc.vector.tensor_scalar(zi, sums[:, :, D:DZ], 1e-6, None, ALU.add).then_inc(z_step, 1)
                if third:
                    dve.wait_ge(rooted, b - 1)
                    at_least(dve, y_ready, b - 3)
                    nc.vector.reciprocal(std_inv[0:NP, w % 2, :], std[0:NP, w % 2, :]).then_inc(std_inverted, 1)
                if first:
                    dve.wait_ge(z_step, 2 * b + 1)
                    nc.vector.reciprocal(zi, zi).then_inc(z_step, 1)
                if third:
                    dve.wait_ge(std_inverted, b - 1)
                    nc.vector.tensor_tensor(shift[0:NP, w % 2, :], minus_mean[0:NP, w, :], std_inv[0:NP, w % 2, :],
                                            ALU.mult).then_inc(coef_ready, 1)
                if first:
                    dve.wait_ge(z_step, 2 * b + 2)
                    if not isinstance(b, int) or b >= 4:
                        wait_batch(dve, y_stored, b - 4, u)
                    nc.vector.tensor_tensor(yb.rearrange("p j (h d) -> p j h d", d=HD),
                                            sums[:, :, 0:D].rearrange("p j (h d) -> p j h d", d=HD),
                                            zi.unsqueeze(3).to_broadcast((NP, BATCH, HEADS, HD)), ALU.mult).then_inc(y_attended, 1)
                if second:
                    dve.wait_ge(squared, b)
                    nc.vector.tensor_reduce(sq_sum[0:NP, v % 2, :], ysq[0:NP, v % 2, :, :], AX_X, ALU.add).then_inc(sq_summed, 1)
                if first:
                    dve.wait_ge(y_attended, b + 1)
                    wait_batch(dve, x_res_in, b, u)
                    nc.vector.tensor_tensor(yb, yb, x_res[0:NP, u, :, :], ALU.add).then_inc(res_added, 1)
                if second:
                    dve.wait_ge(sq_summed, b)
                    at_least(dve, rooted, b - 2)
                    nc.vector.tensor_scalar(var[0:NP, v % 2, :], sq_sum[0:NP, v % 2, :], 1.0 / D, EPS_LN,
                                            ALU.mult, ALU.add).then_inc(var_ready, 1)
                if first:
                    dve.wait_ge(res_added, b + 1)
                    nc.vector.tensor_reduce(y_sum[0:NP, h, :], yb, AX_X, ALU.add).then_inc(y_summed, 1)
                    dve.wait_ge(y_summed, b + 1)
                    nc.vector.tensor_scalar(minus_mean[0:NP, u, :], y_sum[0:NP, h, :], -1.0 / D, None,
                                            ALU.mult).then_inc(mean_ready, 1)

            run_batches(dve, output, BATCHES, 2)


_INS = ['x', 'src', 'dst', 'edge_attr_96', 'L0_gnn_Wq', 'L0_gnn_bq', 'L0_gnn_Wk', 'L0_gnn_bk',
        'L0_gnn_We', 'L0_gnn_be', 'L0_gnn_Wv', 'L0_gnn_bv']


def kernel(**inputs):
    import numpy as _np
    import concourse.bacc as _bacc
    from concourse import mybir as _mybir
    from concourse.bass_utils import run_bass_kernel_spmd as _run

    nc = _bacc.Bacc("TRN2", target_bir_lowering=False, num_devices=1)
    arrays, args = {}, []
    for name in _INS:
        a = _np.ascontiguousarray(inputs[name])
        arrays[f"in_{name}_dram"] = a
        args.append(nc.dram_tensor(f"in_{name}_dram", a.shape, _mybir.dt.from_np(a.dtype), kind="ExternalInput").ap())
    args.append(nc.dram_tensor("out_0_dram", inputs["x"].shape, _mybir.dt.float32, kind="ExternalOutput").ap())
    gnn_kernel(nc, *args)
    r = _run(nc, [arrays], core_ids=[0])
    return r.results[0]["out_0_dram"]
```
